# Optimizing a Trainium2 kernel written in Bass

```python
import numpy as np
import jax
import jax.numpy as jnp

def _softmax(x, axis=-1):
    return jax.nn.softmax(x, axis=axis)

def _gelu(x):
    return jax.nn.gelu(x, approximate=True)

def _silu(x):
    return jax.nn.silu(x)

def _sigmoid(x):
    return jax.nn.sigmoid(x)

def _layernorm(x, axis=-1, eps=1e-05):
    m = jnp.mean(x, axis=axis, keepdims=True)
    v = jnp.var(x, axis=axis, keepdims=True)
    return (x - m) / jnp.sqrt(v + eps)

def _scatter_add(tgt, idx, src, axis=0):
    return tgt.at[idx].add(src)

def _segment_sum(src, seg, n):
    return jax.ops.segment_sum(src, seg, n)
kernel_name = 'mk_xattn_ffn_d1_seqx_r4_3cb367'

def setup_inputs(seed: int=0):
    np.random.seed(seed)
    _w = jnp.asarray

    def _rec_inputs():
        import jax
        import jax.numpy as jnp
        _rk = jax.random.key(seed)
        x = -0.0003929 + 0.9999 * jax.random.normal(jax.random.fold_in(_rk, 1), (4, 1024, 256), jnp.float32)
        _lenS = 1024 - jax.random.randint(jax.random.fold_in(_rk, 7), (4,), 0, max(1, 1024 // 4) + 1, jnp.int32)
        _lenS2 = 77 - jax.random.randint(jax.random.fold_in(_rk, 8), (4,), 0, max(1, 77 // 4) + 1, jnp.int32)
        _ctx_768P = jax.random.normal(jax.random.fold_in(_rk, 11), (4, 16, 192), jnp.float32)
        _ctx_768c = jax.random.dirichlet(jax.random.fold_in(_rk, 511), 0.3 * jnp.ones((16,), jnp.float32), (4, 77))
        _ctx_768t = jnp.einsum('bsk,bkd->bsd', _ctx_768c, _ctx_768P)
        _ctx_768t = _ctx_768t * jax.lax.rsqrt(jnp.mean(jnp.square(_ctx_768t)) + 1e-12) * 0.953939
        ctx_768 = 0.00095986 + 0.999812 * (_ctx_768t + 0.3 * jax.random.normal(jax.random.fold_in(_rk, 611), (4, 77, 192), jnp.float32))
        _validS = jnp.arange(1024)[None, :] < _lenS[:, None]
        _validS2 = jnp.arange(77)[None, :] < _lenS2[:, None]
        _causal = jnp.tril(jnp.ones((1024, 1024), dtype=bool))
        mask_BxS2_bf1 = jnp.ones((4, 77), dtype=bool)
        return (x, ctx_768, mask_BxS2_bf1)
    x, ctx_768, mask_BxS2_bf1 = _rec_inputs()

    def _L0_xattn_setup():
        import jax, jax.numpy as jnp
        import numpy as np
        DIM = 256
        CTX_DIM = 192
        HEADS = 16
        key = jax.random.key(seed)
        ks = jax.random.split(key, 7)
        B, N, M = (4, 1024, 64)
        x = jax.random.normal(ks[0], (B, N, DIM), dtype=jnp.float32)
        context = jax.random.normal(ks[1], (B, M, CTX_DIM), dtype=jnp.float32)
        context_mask = jnp.ones((B, M), dtype=bool)
        s_d = 1.0 / np.sqrt(DIM)
        s_c = 1.0 / np.sqrt(CTX_DIM)
        Wq = jax.random.normal(ks[2], (DIM, DIM), dtype=jnp.float32) * s_d
        Wk = jax.random.normal(ks[3], (CTX_DIM, DIM), dtype=jnp.float32) * s_c
        Wv = jax.random.normal(ks[4], (CTX_DIM, DIM), dtype=jnp.float32) * s_c
        Wo = jax.random.normal(ks[5], (DIM, DIM), dtype=jnp.float32) * s_d
        return {'x': x, 'context': context, 'context_mask': context_mask, 'Wq': Wq, 'Wk': Wk, 'Wv': Wv, 'Wo': Wo}
    _L0_xattn_all = _L0_xattn_setup()
    _L0_xattn_in = {k: v for k, v in _L0_xattn_all.items() if k in ('Wq', 'Wk', 'Wv', 'Wo')}
    del _L0_xattn_all

    def _L0_ffn_setup():
        import jax, jax.numpy as jnp
        import numpy as np
        H = 256
        DFF = 1024
        E_ROUTED = 7
        TOP_K = 2

        def _swiglu(flat, gate_w, up_w, down_w):
            g = flat @ gate_w.T
            up = flat @ up_w.T
            return jax.nn.silu(g) * up @ down_w.T
        key = jax.random.key(seed)
        ks = jax.random.split(key, 8)
        s = 0.02
        return {'x': jax.random.normal(ks[0], (4, 512, H), jnp.float32), 'shared_up': jax.random.normal(ks[1], (DFF, H), jnp.float32) * s, 'shared_gate': jax.random.normal(ks[2], (DFF, H), jnp.float32) * s, 'shared_down': jax.random.normal(ks[3], (H, DFF), jnp.float32) * s, 'routed_up': jax.random.normal(ks[4], (E_ROUTED, DFF, H), jnp.float32) * s, 'routed_gate': jax.random.normal(ks[5], (E_ROUTED, DFF, H), jnp.float32) * s, 'routed_down': jax.random.normal(ks[6], (E_ROUTED, H, DFF), jnp.float32) * s, 'router_w': jax.random.normal(ks[7], (E_ROUTED, H), jnp.float32) * 0.02}
    _L0_ffn_all = _L0_ffn_setup()
    _L0_ffn_in = {k: v for k, v in _L0_ffn_all.items() if k in ('shared_up', 'shared_gate', 'shared_down', 'routed_up', 'routed_gate', 'routed_down', 'router_w')}
    del _L0_ffn_all
    return {'x': x, 'ctx_768': ctx_768, 'mask_BxS2_bf1': mask_BxS2_bf1, 'L0_xattn_Wq': _L0_xattn_in['Wq'], 'L0_xattn_Wk': _L0_xattn_in['Wk'], 'L0_xattn_Wv': _L0_xattn_in['Wv'], 'L0_xattn_Wo': _L0_xattn_in['Wo'], 'L0_ffn_shared_up': _L0_ffn_in['shared_up'], 'L0_ffn_shared_gate': _L0_ffn_in['shared_gate'], 'L0_ffn_shared_down': _L0_ffn_in['shared_down'], 'L0_ffn_routed_up': _L0_ffn_in['routed_up'], 'L0_ffn_routed_gate': _L0_ffn_in['routed_gate'], 'L0_ffn_routed_down': _L0_ffn_in['routed_down'], 'L0_ffn_router_w': _L0_ffn_in['router_w']}

def reference(x, ctx_768, mask_BxS2_bf1, L0_xattn_Wq, L0_xattn_Wk, L0_xattn_Wv, L0_xattn_Wo, L0_ffn_shared_up, L0_ffn_shared_gate, L0_ffn_shared_down, L0_ffn_routed_up, L0_ffn_routed_gate, L0_ffn_routed_down, L0_ffn_router_w):
    import jax
    import jax.numpy as jnp

    def _L0_xattn_ref(x, context, context_mask, Wq, Wk, Wv, Wo):
        import jax, jax.numpy as jnp
        import numpy as np
        DIM = 256
        CTX_DIM = 192
        HEADS = 16
        B, N, _ = x.shape
        M = context.shape[1]
        hd = DIM // HEADS
        scale = hd ** (-0.5)
        q = (x @ Wq).reshape(B, N, HEADS, hd).transpose(0, 2, 1, 3)
        k = (context @ Wk).reshape(B, M, HEADS, hd).transpose(0, 2, 1, 3)
        v = (context @ Wv).reshape(B, M, HEADS, hd).transpose(0, 2, 1, 3)
        scores = jnp.einsum('bhid,bhjd->bhij', q, k) * scale
        max_neg = -jnp.finfo(scores.dtype).max
        scores = jnp.where(context_mask[:, None, None, :], scores, max_neg)
        attn = jax.nn.softmax(scores, axis=-1)
        out = jnp.einsum('bhij,bhjd->bhid', attn, v)
        out = out.transpose(0, 2, 1, 3).reshape(B, N, DIM)
        return out @ Wo

    def _L0_ffn_ref(x, shared_up, shared_gate, shared_down, routed_up, routed_gate, routed_down, router_w):
        import jax, jax.numpy as jnp
        import numpy as np
        H = 256
        DFF = 1024
        E_ROUTED = 7
        TOP_K = 2

        def _swiglu(flat, gate_w, up_w, down_w):
            g = flat @ gate_w.T
            up = flat @ up_w.T
            return jax.nn.silu(g) * up @ down_w.T
        orig_shape = x.shape
        flat = x.reshape(-1, H)
        out = _swiglu(flat, shared_gate, shared_up, shared_down)
        logits = flat @ router_w.T
        probs = jax.nn.softmax(logits, axis=-1)
        top_vals, top_idx = jax.lax.top_k(probs, TOP_K)
        top_vals = top_vals / (top_vals.sum(-1, keepdims=True) + 1e-09)
        combine = jnp.sum(jax.nn.one_hot(top_idx, E_ROUTED, dtype=flat.dtype) * top_vals[..., None], axis=1)
        routed = jnp.zeros_like(flat)
        for e in range(E_ROUTED):
            eo = _swiglu(flat, routed_gate[e], routed_up[e], routed_down[e])
            routed = routed + combine[:, e:e + 1] * eo
        return (out + routed).reshape(orig_shape)
    x = x + _L0_xattn_ref(_layernorm(x, axis=-1), ctx_768, mask_BxS2_bf1, L0_xattn_Wq, L0_xattn_Wk, L0_xattn_Wv, L0_xattn_Wo)
    x = x + _L0_ffn_ref(_layernorm(x, axis=-1), L0_ffn_shared_up, L0_ffn_shared_gate, L0_ffn_shared_down, L0_ffn_routed_up, L0_ffn_routed_gate, L0_ffn_routed_down, L0_ffn_router_w)
    return x

_drawn_inputs = setup_inputs


def setup_inputs(seed=0):
    import zlib

    import numpy as np

    out = dict(_drawn_inputs(seed))
    spreads = {}
    factors = {'L0_ffn_routed_gate': 2.68, 'L0_ffn_router_w': 3.161}
    for name, (base, spread) in spreads.items():
        noise = np.random.default_rng([zlib.crc32(name.encode()), seed]).standard_normal(out[name].shape)
        drawn = base * np.exp(spread * noise) if base else spread * noise
        out[name] = jnp.asarray(drawn.astype(out[name].dtype))
    for name, factor in factors.items():
        out[name] = (out[name] * factor).astype(out[name].dtype)
    return out
```

```python
import concourse.bass as bass
from concourse import mybir
from contextlib import ExitStack

F32 = mybir.dt.float32
F32R = mybir.dt.float32r
I32 = mybir.dt.int32
U8 = mybir.dt.uint8
BF16 = mybir.dt.bfloat16
ACT = mybir.ActivationFunctionType
ALU = mybir.AluOpType
AX = mybir.AxisListType

P = 128
B, N, D = 4, 1024, 256
M, DC = 77, 192
H, HD = 16, 16
F, E = 1024, 7
TOK = B * N
TILES = TOK // P
TPB_LOG = 3
KT = D // P
HH = H // 2
SC = HH * M
CH = -(-SC // P)
SP_ = CH * P
VW = HD + 1
FIRST_HEAD = [c * P // M for c in range(CH)]
HEADS_IN = [min(HH - 1, (c * P + P - 1) // M) - c * P // M + 1 for c in range(CH)]
HMAX = max(HEADS_IN)
BLK = 256
NBLK = TOK // BLK
FT = F // P
WCOLS = 3 * KT * F
EPS_LN = 1e-5
EPS_TOP = 1e-9
UNROLL = 4
LX = 3
PIECE = WCOLS // TILES
WCH = 1024
NW = WCOLS // WCH


CONST_LOADS, CTX_LOADS = 9, 8


def cut(o, n):
    return slice(o, o + n)


def bc(ap, axis, n):
    a = ap.unsqueeze(axis)
    return a.to_broadcast([n if k == axis else s for k, s in enumerate(a.shape)])


def program(nc, x, ctx_t, mask, mask_t, wq, wk, wv, wo, router, experts, ident, head_sel, val_sel, upper,
            expert_no, token_no, pads, out):
    xn2_d = nc.dram_tensor("xn2_d", (TOK + P, D), F32, kind="Internal").ap()
    x1_d = nc.dram_tensor("x1_d", (TOK, D), F32, kind="Internal").ap()
    val_d = nc.dram_tensor("val_d", (B, H * M, VW), F32, kind="Internal").ap()
    table_d = nc.dram_tensor("table_d", (E * TOK, 2), I32, kind="Internal").ap()

    with ExitStack() as stack:
        def sb(name, shape, dt=F32):
            return stack.enter_context(nc.sbuf_tensor(name, shape, dt))

        def sem(name):
            return stack.enter_context(nc.semaphore(name))

        def sems(name, n):
            return [sem(f"{name}{k}") for k in range(n)]

        ident_s = sb("ident_s", [P, P])
        wq_s = sb("wq_s", [P, KT, D])
        wo_s = sb("wo_s", [P, KT, D])
        wr_s = sb("wr_s", [P, KT, E])
        keys = sb("keys", [P, B, KT, SC])
        vals = sb("vals", [P, B, KT, CH * HMAX * VW])
        arena = sb("arena", [P, 5 * FT * P])
        taken = {"A": 0, "B": 0}

        def part(phase, *shape):
            n = 1
            for k in shape:
                n *= k
            o = taken[phase]
            taken[phase] = o + n
            assert taken[phase] <= 5 * FT * P
            ap = arena[:, cut(o, n)]
            if len(shape) == 2:
                ap = ap.rearrange("p (a b) -> p a b", a=shape[0])
            return ap

        xa = part("A", UNROLL, D)
        xr = part("A", 2, D)
        xn = part("A", 2, D)
        xnT = part("A", KT, P)
        qT = part("A", KT, P)
        prob = part("A", KT, SP_)
        probT = part("A", KT, SP_)
        xin = part("B", 2, D)
        x1b = part("B", 2, D)
        y = part("B", 2, D)
        gate = part("B", 2, 2 * BLK)
        hid = part("B", FT, BLK)
        mv1 = sb("mv1", [P, 2, 2])
        mv2 = sb("mv2", [P, 2, 2])
        stat1 = sb("stat1", [P, 2, 6])
        stat2 = sb("stat2", [P, 2, 6])
        smax = sb("smax", [P, KT, HH])
        rsum = sb("rsum", [P, H])
        att = sb("att", [P, D])
        attT = sb("attT", [P, KT, P])
        x1 = sb("x1", [P, 2, D])
        xn2 = sb("xn2", [P, 2, D])
        xn2T = sb("xn2T", [P, KT, P])
        logits = sb("logits", [P, TILES, E])
        zero = sb("zero", [P, D])
        eps_s = sb("eps_s", [P, 1])
        upper_s = sb("upper_s", [P, P], BF16)
        ones_b = sb("ones_b", [P, P], BF16)
        masks_b = sb("masks_b", [P, TILES, E], BF16)
        before_b = sb("before_b", [P, TILES, E], BF16)
        total_b = sb("total_b", [P, E], BF16)
        expert_s = sb("expert_s", [P, 2, E])
        token_s = sb("token_s", [P, TILES + 1], I32)
        pay = sb("pay", [P, 2, TILES, 2], I32)
        pos = sb("pos", [P, 2, TILES], I32)
        counts = sb("counts", [1, 3, 8], I32)
        keys_f = keys[:].rearrange("p b k n -> p (b k n)")

        def route_part(k):
            return keys_f[:, cut(k * TILES * E, TILES * E)].rearrange("p (t e) -> p t e", e=E)

        def route_col(k):
            return keys_f[:, cut(6 * TILES * E + k * TILES, TILES)]

        r_prob, r_sel, r_one, r_two, r_sum, r_pos = (route_part(k) for k in range(6))
        r_a, r_p1, r_p2, r_b, r_w = (route_col(k) for k in range(5))
        raw = sb("raw", [P, WCOLS])
        w_hi = [sb(f"w_hi{k}", [P, WCOLS], F32R) for k in range(2)]
        w_lo = [sb(f"w_lo{k}", [P, WCOLS], F32R) for k in range(2)]
        xT_hi = sb("xT_hi", [P, KT, BLK], F32R)
        xT_lo = sb("xT_lo", [P, KT, BLK], F32R)
        hid_hi = sb("hid_hi", [P, FT, BLK], F32R)
        hid_lo = sb("hid_lo", [P, FT, BLK], F32R)
        slots_g = sb("slots_g", [P, 2, 2], I32)
        slots_s = sb("slots_s", [P, 2, 2], I32)
        ps = stack.enter_context(nc.psum_tensor("ps", [P, 8, 512], F32))
        S0, T0, T1, M1, M2 = 0, 4, 5, 6, 7
        XT_BANK, GATE, UP, Y_BANK, RANK = 0, 1, 3, 5, 7

        ctx_s = raw[:, cut(0, 2 * B * M)].rearrange("p (k n) -> p k n", k=2)
        wkv_s = raw[:, cut(1024, 4 * D)].rearrange("p (w k n) -> p w k n", w=2, k=2)
        keys_m, keep, drop, fill = (raw[:, cut(2048 + 320 * k, B * M)] for k in range(4))
        val_x = raw[:, cut(3400, B * H * VW)].rearrange("p (b n) -> p b n", b=B)
        val_c = raw[:, cut(4500, B * KT * CH * VW)].rearrange("p (b k c w) -> p b k c w", b=B, k=KT, c=CH)
        scratch = sb("scratch", [P, 64])
        count, rcount, ksum, kmean, some, none = (scratch[:, cut(4 * k, 4)] for k in range(6))
        keep_k, keep_v = (scratch[:, cut(32 + 4 * k, 4)] for k in range(2))
        mask_s = sb("mask_s", [P, B * M], U8)
        mask_k = sb("mask_k", [P, B], U8)
        head_s = sb("head_s", [P, HH])
        valsel_s = sb("valsel_s", [P, CH, HMAX])
        upper_f = sb("upper_f", [P, P])

        ld_const, ld_ctx, ld_raw0, ld_pads = sem("ld_const"), sem("ld_ctx"), sem("ld_raw0"), sem("ld_pads")
        dv_zero, st_zero, dv_link, pe_keys, pe_vals, dv_keys = (sem(n) for n in ("dv_zero", "st_zero", "dv_link", "pe_keys", "pe_vals", "dv_keys"))
        dv_valx, st_val, ld_valc, dv_vals, po_vc0, po_pad = (sem(n) for n in ("dv_valx", "st_val", "ld_valc", "dv_vals", "po_vc0", "po_pad"))
        ld_xa, ld_xr = sems("ld_xa", UNROLL), sems("ld_xr", 2)
        st_x1, st_xn2 = sems("st_x1", 2), sems("st_xn2", 2)
        dv_bn1, dv_ag1, dv_bn2, dv_ag2 = (sem(n) for n in ("dv_bn1", "dv_ag1", "dv_bn2", "dv_ag2"))
        ac_ln1, ac_dev1, ac_ln2, ac_dev2 = (sem(n) for n in ("ac_ln1", "ac_dev1", "ac_ln2", "ac_dev2"))
        po_xn, po_xn2, po_whi, po_wlo = (sem(n) for n in ("po_xn", "po_xn2", "po_whi", "po_wlo"))
        pe_xt, pe_qp, pe_ot, pe_wo, pe_x2t, pe_r = (sem(n) for n in ("pe_xt", "pe_qp", "pe_ot", "pe_wo", "pe_x2t", "pe_r"))
        pe_s, pe_eta, pe_etb, pe_pv = (sems(n, 2) for n in ("pe_s", "pe_eta", "pe_etb", "pe_pv"))
        ac_xnt, ac_qt, ac_ont, ac_x2t = (sem(n) for n in ("ac_xnt", "ac_qt", "ac_ont", "ac_x2t"))
        ac_exp, ac_eta = sems("ac_exp", 2), sems("ac_eta", 2)
        dv_max, dv_sub, dv_etb = sems("dv_max", 2), sems("dv_sub", 2), sems("dv_etb", 2)
        dv_rc, dv_norm, dv_x1, dv_l = (sem(n) for n in ("dv_rc", "dv_norm", "dv_x1", "dv_l"))
        dv_shifted, ac_route, dv_masks, pe_rank, dv_pos, dv_counts, st_table = (sem(n) for n in ("dv_shifted", "ac_route", "dv_masks", "pe_rank", "dv_pos", "dv_counts", "st_table"))
        b_xin, b_x1, b_out, b_gather, b_slots_g, b_slots_s, b_add = (sem(n) for n in ("b_xin", "b_x1", "b_out", "b_gather", "b_slots_g", "b_slots_s", "b_add"))
        b_t, b_xhi, b_xlo, b_y, b_ysb = (sem(n) for n in ("b_t", "b_xhi", "b_xlo", "b_y", "b_ysb"))
        b_g, b_u, b_silu, b_h, b_hhi, b_hlo = (sems(n, 4) for n in ("b_g", "b_u", "b_silu", "b_h", "b_hhi", "b_hlo"))
        ld_raw, b_whi, b_wlo = sem("ld_raw"), sem("b_whi"), sem("b_wlo")

        waited = {name: sem(f"{name}_waited") for name in ("DVE", "Pool", "SP")}

        block = stack.enter_context(nc.Block())

        def phase_a(eng, step, first, last, with_batch=False):
            batch = lambda f: [f] if with_batch else []
            lo, hi = UNROLL, TILES - UNROLL
            for i in range(first, lo):
                step(i % UNROLL, lambda o, i=i: 0 <= i + o < TILES, lambda o, i=i: i + o, *batch(lambda o, i=i: (i + o) >> TPB_LOG))
            with eng.Fori(lo // UNROLL, hi // UNROLL) as u:
                t = u * UNROLL
                at = {o: eng.snap(t + o, min_val=lo + o, max_val=hi - UNROLL + o)
                      for o in range(-LX - 1, 2 * UNROLL)}
                if with_batch:
                    of_body = eng.snap(u >> 1, min_val=0, max_val=B - 1)
                    before = eng.snap((t - 1) >> TPB_LOG, min_val=0, max_val=B - 1)
                    batches = {-1: before, **{o: of_body for o in range(UNROLL)}}
                for j in range(UNROLL):
                    step(j, lambda o: True, lambda o, j=j: at[j + o], *batch(lambda o, j=j: batches[j + o]))
            for i in range(hi, last + 1):
                step(i % UNROLL, lambda o, i=i: 0 <= i + o < TILES, lambda o, i=i: i + o, *batch(lambda o, i=i: (i + o) >> TPB_LOG))

        def uses(tile, slot, ring):
            return ((tile - slot) >> (ring.bit_length() - 1)) + 1

        def routed(eng, begin, new_expert, finish):
            g = eng.alloc_register(f"{eng.engine.name}_g")

            def next_block(e, b, was, now):
                n = eng.snap(g, min_val=NBLK + 1, max_val=(E + 1) * NBLK - 1)
                begin(e, b, n, was, now)
                eng.reg_add(g, g, 1)

            def blocks(e, par):
                n = eng.value_load(counts[0:1, 0, bass.ds(e, 1)], min_val=1, max_val=NBLK)
                with eng.Fori(0, 5) as q:
                    with eng.If(q * 3 + 1 < n):
                        with eng.Fori(0, 3) as j:
                            b = eng.snap(q * 3 + j + 1, min_val=1, max_val=NBLK - 1)
                            with eng.If(b < n):
                                next_block(e, b, par, par)
                            eng.nop()
                    eng.nop()

            eng.wait_ge(dv_counts, 1)
            begin(0, 0, NBLK, 0, 1)
            eng.reg_mov(g, NBLK + 1)
            if new_expert:
                new_expert(0, 1, None)
            blocks(0, 1)
            with eng.Fori(0, (E - 1) // 2) as v:
                v = eng.snap(v, min_val=0, max_val=(E - 1) // 2 - 1)
                for k in range(2):
                    e = eng.snap(v * 2 + (1 + k), min_val=1 + k, max_val=E - 2 + k)
                    next_block(e, 0, 1 - k, k)
                    if new_expert:
                        new_expert(e, k, v)
                    blocks(e, k)
            finish(eng.snap(g, min_val=NBLK + E, max_val=(E + 1) * NBLK))

        def apart(eng):
            eng.sem_inc(waited[eng.engine.name], 1)

        def rows(ap, r, n=2):
            return ap[bass.ds(r, n * P), :].rearrange("(t p) d -> p t d", p=P)

        @block.sync
        def _(sp):
            for dst, src in ((ident_s[:], ident), (wq_s[:], wq), (wo_s[:], wo), (wr_s[:], router),
                             (head_s[:], head_sel), (valsel_s[:], val_sel), (upper_f[:], upper),
                             (expert_s[:], expert_no), (token_s[:], token_no)):
                sp.dma_start(dst, src).then_inc(ld_const, 16)
            for i in range(UNROLL):
                sp.dma_start(xa[:, i, :], x[cut(i * P, P), :]).then_inc(ld_xa[i], 16)
            sp.dma_start(table_d, pads).then_inc(ld_pads, 16)
            sp.wait_ge(dv_zero, 1)
            sp.dma_start(xn2_d[cut(TOK, P), :], zero[:]).then_inc(st_zero, 16)
            sp.dma_start(out[cut(TOK, P), :], zero[:]).then_inc(st_zero, 16)
            sp.wait_ge(dv_valx, 1)
            for b in range(B):
                sp.dma_start(val_d[b].rearrange("(h k) c -> k h c", k=M),
                             val_x[0:M, b, :].rearrange("k (h c) -> k h c", h=H)).then_inc(st_val, 16)
            sp.wait_ge(st_val, 16 * B)
            sp.wait_ge(po_vc0, 1)
            full = (CH - 1) * P
            for b in range(B):
                for h in range(KT):
                    sp.dma_start(val_c[:, b, h, 0:CH - 1, :],
                                 val_d[b, cut(h * SC, full), :].rearrange("(c p) w -> p c w", p=P)).then_inc(ld_valc, 16)
                    sp.dma_start(val_c[0:SC - full, b, h, CH - 1, :],
                                 val_d[b, cut(h * SC + full, SC - full), :]).then_inc(ld_valc, 16)
            sp.wait_ge(dv_vals, 1)
            sp.dma_start(raw[:], experts[0]).then_inc(ld_raw0, 16)

            def step(s, has, tile):
                if has(-2):
                    sp.wait_ge(dv_x1, tile(-2) + 1)
                if has(0):
                    sp.dma_start(xr[:, s % 2, :], x[bass.ds(tile(0) * P, P), :]).then_inc(ld_xr[s % 2], 16)
                if has(-2):
                    sp.dma_start(x1_d[bass.ds(tile(-2) * P, P), :], x1[:, s % 2, :]).then_inc(st_x1[s % 2], 16)
                    sp.wait_ge(po_xn2, tile(-2) + 1)
                    sp.dma_start(xn2_d[bass.ds(tile(-2) * P, P), :], xn2[:, s % 2, :]).then_inc(st_xn2[s % 2], 16)
                if has(0) and has(UNROLL):
                    sp.wait_ge(po_xn, tile(0) + 1)
                    sp.dma_start(xa[:, s, :], x[bass.ds(tile(UNROLL) * P, P), :]).then_inc(ld_xa[s], 16)

            phase_a(sp, step, 0, TILES + 1)
            for k in range(2):
                sp.wait_ge(st_x1[k], 16 * (TILES // 2))
                sp.wait_ge(st_xn2[k], 16 * (TILES // 2))
            sp.wait_ge(st_zero, 32)
            sp.dma_start(xin[:], rows(xn2_d, 0)).then_inc(b_xin, 16)
            sp.dma_start(x1b[:], rows(x1_d, 0)).then_inc(b_x1, 16)
            sp.wait_ge(po_wlo, TILES)
            sp.dma_start(raw[:], experts[1]).then_inc(ld_raw, 16)

            sp.wait_ge(b_t, 1)
            sp.dma_start(xin[:], rows(xn2_d, BLK)).then_inc(b_xin, 16)
            with sp.Fori(1, NBLK - 1) as n:
                n = sp.snap(n, min_val=1, max_val=NBLK - 2)
                sp.wait_ge(b_ysb, n)
                sp.dma_start(rows(out, (n - 1) * BLK), y[:]).then_inc(b_out, 16)
                sp.dma_start(x1b[:], rows(x1_d, n * BLK)).then_inc(b_x1, 16)
                sp.wait_ge(b_t, n + 1)
                sp.dma_start(xin[:], rows(xn2_d, (n + 1) * BLK)).then_inc(b_xin, 16)
            sp.wait_ge(b_ysb, NBLK - 1)
            sp.dma_start(rows(out, (NBLK - 2) * BLK), y[:]).then_inc(b_out, 16)
            sp.dma_start(x1b[:], rows(x1_d, (NBLK - 1) * BLK)).then_inc(b_x1, 16)

            last_row = sp.alloc_register("sp_last_row")

            def begin(e, b, g, was, now):
                if isinstance(g, int):
                    sp.wait_ge(st_table, 16 * 2 * TILES)
                    sp.dma_start(slots_g[:], rows(table_d, 0)).then_inc(b_slots_g, 16)
                    sp.wait_ge(b_ysb, NBLK)
                    sp.dma_start(rows(out, (NBLK - 1) * BLK), y[:]).then_inc(b_out, 16)
                    sp.reg_mov(last_row, 0)
                    return
                row = sp.snap(e * TOK + b * BLK, min_val=BLK, max_val=E * TOK - BLK)
                sp.wait_ge(b_gather, (g - NBLK) * 32)
                sp.dma_start(slots_g[:], rows(table_d, row)).then_inc(b_slots_g, 16)
                end(g)
                sp.reg_mov(last_row, row)

            def end(g):
                before = sp.snap(last_row, min_val=0, max_val=E * TOK - BLK)
                sp.wait_ge(b_add, (g - NBLK) * 32)
                sp.dma_start(slots_s[:], rows(table_d, before)).then_inc(b_slots_s, 16)

            def finish(g):
                end(g)
                sp.wait_ge(b_out, 16 * NBLK)
                sp.wait_ge(b_add, (g - NBLK) * 32 + 32)
                apart(sp)

            routed(sp, begin, None, finish)

        @block.gpsimd
        def _(po):
            def normalise(dst, src, mv):
                return po.tensor_scalar(dst, src, mv[:, 0:1], mv[:, 1:2], ALU.subtract, ALU.mult)

            po.memset(prob[:, :, SC:], 0.0).then_inc(po_pad, 1)
            po.memset(val_c, 0.0).then_inc(po_vc0, 1)

            def step(s, has, tile):
                if has(2):
                    po.wait_ge(ac_dev1, tile(2) + 1)
                    if has(0):
                        po.wait_ge(pe_xt, tile(0) + 1)
                    apart(po)
                    normalise(xn[:, s % 2, :], xa[:, (s + 2) % UNROLL, :], mv1[:, s % 2, :]).then_inc(po_xn, 1)
                if has(-2):
                    o = tile(-2) * PIECE
                    if isinstance(o, int) and o == 0:
                        po.wait_ge(ld_raw0, 16)
                    po.tensor_copy(w_hi[0][:, bass.ds(o, PIECE)], raw[:, bass.ds(o, PIECE)]).then_inc(po_whi, 1)
                if has(-2):
                    po.wait_ge(ac_dev2, tile(-2) + 1)
                    if has(-4):
                        po.wait_ge(pe_x2t, tile(-4) + 1)
                        po.wait_ge(st_xn2[s % 2], uses(tile(-4), s % 2, 2) * 16)
                    apart(po)
                    normalise(xn2[:, s % 2, :], x1[:, s % 2, :], mv2[:, s % 2, :]).then_inc(po_xn2, 1)
                if has(-2):
                    po.wait_ge(po_whi, tile(-2) + 1)
                    po.tensor_tensor(w_lo[0][:, bass.ds(o, PIECE)], raw[:, bass.ds(o, PIECE)],
                                     w_hi[0][:, bass.ds(o, PIECE)].bitcast(F32), ALU.subtract).then_inc(po_wlo, 1)

            phase_a(po, step, -2, TILES + 1)

            po.wait_ge(dv_pos, 1)
            po.wait_ge(ld_pads, 16)
            for t in range(TILES):
                for k in range(2):
                    po.indirect_dma_start(out=table_d, out_offset=bass.IndirectOffsetOnAxis(ap=pos[:, k, t:t + 1], axis=0),
                                          in_=pay[:, k, t, :], in_offset=None).then_inc(st_table, 16)

            def begin(e, b, g, was, now):
                r = g - NBLK
                po.wait_ge(b_slots_g, r * 16 + 16)
                po.wait_ge(b_t, g)
                apart(po)
                for t in range(2):
                    po.indirect_dma_start(out=xin[:, t, :], out_offset=None, in_=xn2_d,
                                          in_offset=bass.IndirectOffsetOnAxis(ap=slots_g[:, t, 0:1], axis=0)).then_inc(b_gather, 16)
                if not isinstance(g, int):
                    add(g)

            def add(g):
                r = g - NBLK
                po.wait_ge(b_ysb, g)
                for t in range(2):
                    po.wait_ge(b_add, r * 32 + 16 * t)
                    apart(po)
                    po.indirect_dma_start(out=out, out_offset=bass.IndirectOffsetOnAxis(ap=slots_s[:, t, 0:1], axis=0),
                                          in_=y[:, t, :], in_offset=None, compute_op=ALU.add).then_inc(b_add, 16)

            def first_expert(e, par, v):
                if v is None:
                    po.wait_ge(b_out, 16 * NBLK)
                    po.wait_ge(st_zero, 32)
                    for t in range(2):
                        if t:
                            po.wait_ge(b_add, 16)
                        po.indirect_dma_start(out=out, out_offset=bass.IndirectOffsetOnAxis(ap=token_s[:, TILES:TILES + 1], axis=0),
                                              in_=zero[:], in_offset=None, compute_op=ALU.add).then_inc(b_add, 16)

            routed(po, begin, first_expert, add)

        @block.tensor
        def _(pe):
            mm = nc.tensor.matmul

            pe.wait_ge(ld_ctx, 16 * CTX_LOADS)
            for h in range(KT):
                for k, kp in ((0, P), (1, DC - P)):
                    last = mm(ps[:, h, 0:B * M], wkv_s[0:kp, 0, k, cut(h * P, P)], ctx_s[0:kp, k, :],
                              start=k == 0, stop=k == 1)
            last.then_inc(pe_keys, 1)
            for b in range(B):
                for k, kp in ((0, P), (1, DC - P)):
                    last = mm(ps[0:M, 2 + b, 0:D], ctx_s[0:kp, k, cut(b * M, M)], wkv_s[0:kp, 1, k, :],
                              start=k == 0, stop=k == 1)
            last.then_inc(pe_vals, 1)
            pe.wait_ge(ld_const, 16 * CONST_LOADS)
            pe.wait_ge(po_pad, 1)

            def transpose_probs(half):
                for c in range(CH):
                    bank, col = (T0, c * P) if c < 3 else (T1, (c - 3) * P)
                    i = nc.tensor.transpose(ps[:, bank, cut(col, P)], prob[:, half, cut(c * P, P)], ident_s[:])
                    if c == 2:
                        i.then_inc(pe_eta[half], 1)
                i.then_inc(pe_etb[half], 1)

            def attend(half, batch):
                for c in range(CH):
                    n = HEADS_IN[c] * VW
                    i = mm(ps[:, M2, cut((half * HH + FIRST_HEAD[c]) * VW, n)], probT[:, half, cut(c * P, P)],
                           vals[:, batch, half, cut(c * HMAX * VW, n)] if isinstance(batch, int) else
                           vals[:, bass.ds(batch, 1), half, cut(c * HMAX * VW, n)],
                           start=half == 0 and c == 0, stop=half == 1 and c == CH - 1, skip_group_check=True)
                i.then_inc(pe_pv[half], 1)

            def score(half, batch):
                for q in range(2):
                    n = SC // 2
                    i = mm(ps[:, S0 + 2 * half + q, 0:n], qT[:, half, :],
                           keys[:, batch, half, cut(q * n, n)] if isinstance(batch, int) else
                           keys[:, bass.ds(batch, 1), half, cut(q * n, n)], start=True, stop=True)
                i.then_inc(pe_s[half], 1)

            def transpose_rows(dst, src):
                for k in range(KT):
                    i = nc.tensor.transpose(dst[:, cut(k * P, P)], src[:, cut(k * P, P)], ident_s[:])
                return i

            def step(s, has, tile, batch):
                if has(-1):
                    before = batch(-1)
                    pe.wait_ge(ac_exp[1], tile(-1) + 1)
                    pe.wait_ge(ac_eta[0], tile(-1) + 1)
                    pe.wait_ge(dv_etb[0], tile(-1) + 1)
                    transpose_probs(1)
                if has(-LX):
                    pe.wait_ge(po_xn2, tile(-LX) + 1)
                    if has(0):
                        pe.wait_ge(ac_qt, tile(0) + 1)
                    transpose_rows(ps[:, M1, 0:D], xn2[:, (s - LX) % 2, :]).then_inc(pe_x2t, 1)
                if has(-1):
                    if has(-2):
                        pe.wait_ge(dv_x1, tile(-2) + 1)
                    if has(-LX - 1):
                        pe.wait_ge(dv_l, tile(-LX - 1) + 1)
                    if isinstance(before, int) and tile(-1) == 0:
                        pe.wait_ge(dv_vals, 1)
                    attend(0, before)
                if has(0):
                    now = batch(0)
                    pe.wait_ge(ac_qt, tile(0) + 1)
                    if isinstance(now, int) and tile(0) == 0:
                        pe.wait_ge(dv_keys, 1)
                        pe.wait_ge(dv_valx, 1)
                    score(0, now)
                if has(-1):
                    pe.wait_ge(ac_eta[1], tile(-1) + 1)
                    pe.wait_ge(dv_etb[1], tile(-1) + 1)
                    attend(1, before)
                if has(1):
                    pe.wait_ge(po_xn, tile(1) + 1)
                    if has(-LX):
                        pe.wait_ge(ac_x2t, tile(-LX) + 1)
                    transpose_rows(ps[:, M1, 0:D], xn[:, (s + 1) % 2, :]).then_inc(pe_xt, 1)
                if has(0):
                    score(1, now)
                if has(1):
                    pe.wait_ge(ac_xnt, tile(1) + 1)
                    for h in range(KT):
                        for k in range(KT):
                            last = mm(ps[:, M1, cut(D + h * P, P)], wq_s[:, k, cut(h * P, P)], xnT[:, k, :],
                                      start=k == 0, stop=k == KT - 1)
                    last.then_inc(pe_qp, 1)
                if has(-1):
                    pe.wait_ge(dv_norm, tile(-1) + 1)
                    transpose_rows(ps[:, T1, D:2 * D], att[:]).then_inc(pe_ot, 1)
                if has(0):
                    pe.wait_ge(ac_exp[0], tile(0) + 1)
                    if has(-1):
                        pe.wait_ge(ac_ont, tile(-1) + 1)
                    transpose_probs(0)
                if has(-1):
                    pe.wait_ge(ac_ont, tile(-1) + 1)
                    for k in range(KT):
                        last = mm(ps[:, M2, 0:D], attT[:, k, :], wo_s[:, k, :], start=k == 0, stop=k == KT - 1)
                    last.then_inc(pe_wo, 1)
                if has(-LX):
                    pe.wait_ge(ac_x2t, tile(-LX) + 1)
                    if not has(-1):
                        if has(-LX - 1):
                            pe.wait_ge(dv_l, tile(-LX - 1) + 1)
                            pe.wait_ge(dv_x1, tile(-2) + 1 if has(-2) else TILES)
                    for k in range(KT):
                        last = mm(ps[:, M2, cut(2 * D - 8, E)], xn2T[:, k, :], wr_s[:, k, :],
                                  start=k == 0, stop=k == KT - 1)
                    last.then_inc(pe_r, 1)

            phase_a(pe, step, -1, TILES + LX - 1, with_batch=True)

            def transpose_block(g, wait):
                wait()
                if not (isinstance(g, int) and g == 0):
                    pe.wait_ge(b_xlo, g)
                for k in range(KT):
                    for t in range(2):
                        i = nc.tensor.transpose(ps[:, XT_BANK, cut(k * BLK + t * P, P)], xin[:, t, cut(k * P, P)], ident_s[:])
                i.then_inc(b_t, 1)

            def down(g, par):
                if not (isinstance(g, int) and g == 1):
                    pe.wait_ge(b_ysb, g - 1)
                for p in range(4):
                    pe.wait_ge(b_hhi[p], g)
                    pe.wait_ge(b_hlo[p], g)
                    for t in range(2):
                        for f in (2 * p, 2 * p + 1):
                            o = 2 * KT * F + f * D
                            for n, (a, w) in enumerate(((hid_hi, w_hi), (hid_lo, w_hi), (hid_hi, w_lo))):
                                i = mm(ps[:, Y_BANK + t, 0:D], a[:, f, cut(t * P, P)], w[par][:, cut(o, D)],
                                       start=f == 0 and n == 0, stop=f == FT - 1 and n == 2)
                i.then_inc(b_y, 1)

            def gate_up(g, par):
                pe.wait_ge(b_xlo, g + 1)
                for p in range(4):
                    if p >= 2:
                        pe.wait_ge(b_h[p - 2], g + 1)
                    for m, (bank, ready) in enumerate(((GATE + p % 2, b_g[p]), (UP + p % 2, b_u[p]))):
                        for f in range(2):
                            for k in range(KT):
                                o = (m * KT + k) * F + (2 * p + f) * P
                                for n, (w, a) in enumerate(((w_hi, xT_hi), (w_hi, xT_lo), (w_lo, xT_hi))):
                                    i = mm(ps[:, bank, cut(f * BLK, BLK)], w[par][:, cut(o, P)], a[:, k, :],
                                           start=k == 0 and n == 0, stop=k == KT - 1 and n == 2)
                        i.then_inc(ready, 1)

            def shared(g):
                transpose_block(g, lambda: pe.wait_ge(b_xin, g * 16 + 16))
                if not (isinstance(g, int) and g == 0):
                    down(g, 0)
                gate_up(g, 0)

            pe.wait_ge(po_wlo, TILES)
            shared(0)
            shared(1)
            pe.wait_ge(dv_masks, 1)
            mm(ps[:, RANK, 0:TILES * E], upper_s[:], masks_b[:].rearrange("p t e -> p (t e)"), start=True, stop=False)
            mm(ps[:, RANK, 0:TILES * E], ones_b[:], before_b[:].rearrange("p t e -> p (t e)"), start=False, stop=True)
            mm(ps[:, RANK, cut(TILES * E, E)], ones_b[:], total_b[:], start=True, stop=True).then_inc(pe_rank, 1)
            with pe.Fori(2, NBLK) as g:
                shared(pe.snap(g, min_val=2, max_val=NBLK - 1))

            def begin(e, b, g, was, now):
                transpose_block(g, lambda: pe.wait_ge(b_gather, (g - NBLK) * 32 + 32))
                down(g, was)
                if isinstance(b, int):
                    pe.wait_ge(b_wlo, (e + 1) * NW)
                gate_up(g, now)

            routed(pe, begin, None, lambda g: down(g, 1))

        @block.scalar
        def _(ac):
            for dst, src in ((ctx_s[:, 0, :], ctx_t[0:P, :]), (ctx_s[0:DC - P, 1, :], ctx_t[P:DC, :]),
                             (wkv_s[:, 0, 0, :], wk[0:P, :]), (wkv_s[0:DC - P, 0, 1, :], wk[P:DC, :]),
                             (wkv_s[:, 1, 0, :], wv[0:P, :]), (wkv_s[0:DC - P, 1, 1, :], wv[P:DC, :]),
                             (mask_s[:], mask.rearrange("b k -> (b k)").unsqueeze(0).partition_broadcast(P)),
                             (mask_k[0:M, :], mask_t)):
                ac.dma_start(dst, src).then_inc(ld_ctx, 16)

            def copy(dst, src):
                return nc.scalar.activation(dst, src, ACT.Copy)

            def soften(half, n):
                ac.wait_ge(dv_sub[half], n)
                nc.scalar.activation(prob[:, half, 0:SC], prob[:, half, 0:SC], ACT.Exp, scale=HD ** -0.5).then_inc(ac_exp[half], 1)

            def probs_a(half, n):
                ac.wait_ge(pe_eta[half], n)
                copy(probT[:, half, 0:3 * P], ps[:, T0, 0:3 * P]).then_inc(ac_eta[half], 1)

            def deviation(mv, s_ag, s_ln, s_dev, n):
                ac.wait_ge(s_ag, n)
                nc.scalar.activation(mv[:, 1:2], mv[:, 1:2], ACT.Ln, bias=eps_s[:]).then_inc(s_ln, 1)
                ac.wait_ge(s_ln, n)
                nc.scalar.activation(mv[:, 1:2], mv[:, 1:2], ACT.Exp, scale=-0.5).then_inc(s_dev, 1)

            ac.wait_ge(dv_zero, 1)

            def step(s, has, tile):
                if has(-1):
                    probs_a(1, tile(-1) + 1)
                if has(-2):
                    deviation(mv2[:, s % 2, :], dv_ag2, ac_ln2, ac_dev2, tile(-2) + 1)
                if has(-LX):
                    ac.wait_ge(pe_x2t, tile(-LX) + 1)
                    copy(xn2T[:].rearrange("p k n -> p (k n)"), ps[:, M1, 0:D]).then_inc(ac_x2t, 1)
                if has(1):
                    ac.wait_ge(pe_xt, tile(1) + 1)
                    copy(xnT[:].rearrange("p k n -> p (k n)"), ps[:, M1, 0:D]).then_inc(ac_xnt, 1)
                if has(0):
                    soften(0, tile(0) + 1)
                if has(1):
                    ac.wait_ge(pe_qp, tile(1) + 1)
                    copy(qT[:].rearrange("p k n -> p (k n)"), ps[:, M1, D:2 * D]).then_inc(ac_qt, 1)
                if has(-1):
                    ac.wait_ge(pe_ot, tile(-1) + 1)
                    copy(attT[:].rearrange("p k n -> p (k n)"), ps[:, T1, D:2 * D]).then_inc(ac_ont, 1)
                if has(2):
                    deviation(mv1[:, s % 2, :], dv_ag1, ac_ln1, ac_dev1, tile(2) + 1)
                if has(0):
                    soften(1, tile(0) + 1)
                    probs_a(0, tile(0) + 1)

            phase_a(ac, step, -2, TILES + LX - 1)

            def act_block(g):
                ac.wait_ge(b_t, g + 1)
                copy(xT_hi[:].rearrange("p k n -> p (k n)"), ps[:, XT_BANK, :]).then_inc(b_xhi, 1)

                def high(p):
                    ac.wait_ge(b_h[p], g + 1)
                    copy(hid_hi[:, cut(2 * p, 2), :], hid[:, cut(2 * p, 2), :]).then_inc(b_hhi[p], 1)

                for p in range(4):
                    ac.wait_ge(b_g[p], g + 1)
                    if p >= 2:
                        ac.wait_ge(b_h[p - 2], g + 1)
                    nc.scalar.activation(gate[:, p % 2, :], ps[:, GATE + p % 2, :], ACT.Silu).then_inc(b_silu[p], 1)
                    if p:
                        high(p - 1)
                high(3)

            def high_weights(at, par):
                ac.wait_ge(ld_raw, at * 16)
                for c in range(NW):
                    copy(w_hi[par][:, cut(c * WCH, WCH)], raw[:, cut(c * WCH, WCH)]).then_inc(b_whi, 1)

            def load_raw(at):
                ac.wait_ge(b_wlo, (at - 1) * NW)
                if not isinstance(at, int):
                    at = nc.s_assert_within(at, 0, E, skip_runtime_bounds_check_because="the last body's load is left out")
                ac.dma_start(raw[:], experts[bass.ds(at, 1)].rearrange("a p n -> p (a n)")).then_inc(ld_raw, 16)

            act_block(0)
            high_weights(1, 1)
            load_raw(2)
            ac.wait_ge(dv_shifted, 1)
            nc.scalar.activation(r_prob, r_prob, ACT.Exp).then_inc(ac_route, 1)
            with ac.Fori(1, NBLK) as g:
                act_block(ac.snap(g, min_val=1, max_val=NBLK - 1))

            def new_expert(e, par, v):
                if v is None:
                    high_weights(e + 2, 1 - par)
                    load_raw(e + 3)
                elif par == 0:
                    high_weights(e + 2, 1)
                    with ac.If(v < 2):
                        load_raw(e + 3)
                    ac.nop()
                else:
                    with ac.If(v < 2):
                        high_weights(e + 2, 0)
                        load_raw(e + 3)
                    ac.nop()

            routed(ac, lambda e, b, g, was, now: act_block(g), new_expert, lambda g: None)

        @block.vector
        def _(dv):
            V = nc.vector
            links = [0]

            def link(i):
                links[0] += 1
                i.then_inc(dv_link, 1)
                dv.wait_ge(dv_link, links[0])

            V.memset(eps_s[:], EPS_LN)
            V.memset(zero[:], 0.0).then_inc(dv_zero, 1)
            V.memset(ones_b[:], 1.0)
            dv.wait_ge(ld_const, 16 * CONST_LOADS)
            V.tensor_copy(upper_s[:], upper_f[:])

            def key_values():
                dv.wait_ge(ld_ctx, 16 * CTX_LOADS)
                V.tensor_copy(keep_k[0:M], mask_k[0:M])
                link(V.tensor_copy(keep, mask_s[:]))
                V.tensor_scalar(drop, keep, -1.0, 1.0, ALU.mult, ALU.add)
                link(V.tensor_reduce(count, keep.rearrange("p (b k) -> p b k", b=B), AX.X, ALU.add))
                V.tensor_scalar(some, count, 1.0, None, ALU.min)
                link(V.tensor_scalar(count, count, 1.0, None, ALU.max))
                V.reciprocal(rcount, count)
                link(V.tensor_scalar(none, some, -1.0, 1.0, ALU.mult, ALU.add))
                link(V.tensor_tensor(keep_v[0:M], keep_k[0:M], none[0:M], ALU.max))
                dv.wait_ge(pe_keys, 1)
                for h in range(KT):
                    link(V.tensor_tensor(keys_m, ps[:, h, 0:B * M], keep, ALU.mult))
                    per_batch = keys_m.rearrange("p (b k) -> p b k", b=B)
                    link(V.tensor_reduce(ksum, per_batch, AX.X, ALU.add))
                    link(V.tensor_tensor(kmean, ksum, rcount, ALU.mult))
                    link(V.tensor_tensor(fill.rearrange("p (b k) -> p b k", b=B), drop.rearrange("p (b k) -> p b k", b=B),
                                         bc(kmean, 2, M), ALU.mult))
                    link(V.tensor_tensor(keys_m, keys_m, fill, ALU.add))
                    for b in range(B):
                        i = V.tensor_tensor(keys[:, b, h, :].rearrange("p (h k) -> p h k", h=HH),
                                            bc(keys_m[:, cut(b * M, M)], 1, HH), bc(head_s[:], 2, M), ALU.mult)
                    link(i)
                V.tensor_copy(scratch[:, 63:64], kmean[:, 0:1]).then_inc(dv_keys, 1)
                dv.wait_ge(pe_vals, 1)
                for b in range(B):
                    by_head = val_x[0:M, b, :].rearrange("k (h c) -> k h c", h=H)
                    V.tensor_scalar(by_head[:, :, 0:HD], ps[0:M, 2 + b, 0:D].rearrange("k (h c) -> k h c", h=H),
                                    keep_v[0:M, b:b + 1], None, ALU.mult)
                    i = V.tensor_copy(by_head[:, :, HD], keep_v[0:M, b:b + 1].to_broadcast([M, H]))
                i.then_inc(dv_valx, 1)

            def chunk_values():
                dv.wait_ge(ld_valc, 16 * B * KT * 2)
                for b in range(B):
                    for h in range(KT):
                        i = V.tensor_tensor(vals[:, b, h, :].rearrange("p (c j w) -> p c j w", c=CH, j=HMAX),
                                            bc(val_c[:, b, h], 2, HMAX), bc(valsel_s[:], 3, VW), ALU.mult)
                i.then_inc(dv_vals, 1)

            def norm_stats(src, stat, mv, s_bn, s_ag, n):
                V.bn_stats(stat, src).then_inc(s_bn, 1)
                dv.wait_ge(s_bn, n)
                apart(dv)
                V.bn_aggr(mv, stat).then_inc(s_ag, 1)

            def shift(half, n):
                scores = ps[:, cut(S0 + 2 * half, 2), 0:SC // 2].rearrange("p q (h k) -> p q h k", k=M)
                top = smax[:, half, :].rearrange("p (q h) -> p q h", q=2)
                dv.wait_ge(pe_s[half], n)
                V.tensor_reduce(top, scores, AX.X, ALU.max).then_inc(dv_max[half], 1)
                dv.wait_ge(dv_max[half], n)
                V.tensor_tensor(prob[:, half, 0:SC].rearrange("p (q h k) -> p q h k", q=2, k=M), scores,
                                bc(top, 3, M), ALU.subtract).then_inc(dv_sub[half], 1)

            def probs_b(half, n):
                dv.wait_ge(pe_etb[half], n)
                V.tensor_copy(probT[:, half, 3 * P:], ps[:, T1, 0:2 * P]).then_inc(dv_etb[half], 1)

            def step(s, has, tile):
                if has(-2):
                    n = tile(-2) + 1
                    dv.wait_ge(ld_xr[s % 2], uses(tile(-2), s % 2, 2) * 16)
                    if has(-4):
                        dv.wait_ge(st_x1[s % 2], uses(tile(-4), s % 2, 2) * 16)
                        dv.wait_ge(po_xn2, tile(-4) + 1)
                    dv.wait_ge(pe_wo, n)
                    if has(-LX - 1):
                        dv.wait_ge(pe_r, tile(-LX - 1) + 1)
                    V.tensor_tensor(x1[:, s % 2, :], ps[:, M2, 0:D], xr[:, s % 2, :], ALU.add).then_inc(dv_x1, 1)
                if has(-LX - 1):
                    if not has(-2):
                        dv.wait_ge(pe_r, tile(-LX - 1) + 1)
                    V.tensor_copy(logits[:, bass.ds(tile(-LX - 1), 1), :].rearrange("p a e -> p (a e)"),
                                  ps[:, M2, cut(2 * D - 8, E)]).then_inc(dv_l, 1)
                if has(-2):
                    dv.wait_ge(dv_x1, n)
                    norm_stats(x1[:, s % 2, :], stat2[:, s % 2, :], mv2[:, s % 2, :], dv_bn2, dv_ag2, n)
                if has(-1):
                    probs_b(1, tile(-1) + 1)
                if has(0):
                    shift(0, tile(0) + 1)
                if has(-1):
                    heads = ps[:, M2, 0:H * VW].rearrange("p (h c) -> p h c", h=H)
                    dv.wait_ge(pe_pv[1], tile(-1) + 1)
                    V.reciprocal(rsum[:], heads[:, :, HD]).then_inc(dv_rc, 1)
                    dv.wait_ge(dv_rc, tile(-1) + 1)
                    V.tensor_tensor(att[:].rearrange("p (h c) -> p h c", h=H), heads[:, :, 0:HD],
                                    bc(rsum[:], 2, HD), ALU.mult).then_inc(dv_norm, 1)
                if has(2):
                    n = tile(2) + 1
                    dv.wait_ge(ld_xa[(s + 2) % UNROLL], uses(tile(2), (s + 2) % UNROLL, UNROLL) * 16)
                    if has(0):
                        dv.wait_ge(po_xn, tile(0) + 1)
                    norm_stats(xa[:, (s + 2) % UNROLL, :], stat1[:, s % 2, :], mv1[:, s % 2, :], dv_bn1, dv_ag1, n)
                if has(0):
                    shift(1, tile(0) + 1)
                    probs_b(0, tile(0) + 1)

            for i in (-2, -1):
                step(i % UNROLL, lambda o, i=i: 0 <= i + o < TILES, lambda o, i=i: i + o)
            key_values()
            chunk_values()
            phase_a(dv, step, 0, TILES + LX)

            def block_of(g, finish):
                dv.wait_ge(b_xhi, g + 1)
                V.tensor_tensor(xT_lo[:].rearrange("p k n -> p (k n)"), ps[:, XT_BANK, :],
                                xT_hi[:].rearrange("p k n -> p (k n)").bitcast(F32), ALU.subtract).then_inc(b_xlo, 1)
                if finish:
                    finish(g)

                def low(p):
                    dv.wait_ge(b_hhi[p], g + 1)
                    pair = cut(2 * p, 2)
                    V.tensor_tensor(hid_lo[:, pair, :], hid[:, pair, :], hid_hi[:, pair, :].bitcast(F32),
                                    ALU.subtract).then_inc(b_hlo[p], 1)

                for p in range(4):
                    dv.wait_ge(b_silu[p], g + 1)
                    dv.wait_ge(b_u[p], g + 1)
                    V.tensor_tensor(hid[:, cut(2 * p, 2), :].rearrange("p f n -> p (f n)"), gate[:, p % 2, :],
                                    ps[:, UP + p % 2, :], ALU.mult).then_inc(b_h[p], 1)
                    if p:
                        low(p - 1)
                low(3)

            def end_shared(g):
                dv.wait_ge(b_y, g)
                dv.wait_ge(b_x1, g * 16)
                if not (isinstance(g, int) and g == 1):
                    dv.wait_ge(b_out, g * 16 - 16)
                V.tensor_tensor(y, ps[:, cut(Y_BANK, 2), 0:D], x1b, ALU.add).then_inc(b_ysb, 1)

            def end_routed(g):
                dv.wait_ge(b_y, g)
                dv.wait_ge(b_slots_s, (g - NBLK) * 16)
                dv.wait_ge(b_add, (g - NBLK) * 32)
                for t in range(2):
                    i = V.tensor_scalar(y[:, t, :], ps[:, Y_BANK + t, 0:D], slots_s[:, t, 1:2].bitcast(F32), None, ALU.mult)
                i.then_inc(b_ysb, 1)

            def low_weights(at, par):
                for c in range(NW):
                    dv.wait_ge(b_whi, (at - 1) * NW + c + 1)
                    V.tensor_tensor(w_lo[par][:, cut(c * WCH, WCH)], raw[:, cut(c * WCH, WCH)],
                                    w_hi[par][:, cut(c * WCH, WCH)].bitcast(F32), ALU.subtract).then_inc(b_wlo, 1)

            def choose():
                rank = bc(expert_s[:, 1, :], 1, TILES)
                link(V.tensor_reduce(r_a, logits[:], AX.X, ALU.max))
                V.tensor_tensor(r_prob, logits[:], bc(r_a, 2, E), ALU.subtract).then_inc(dv_shifted, 1)
                dv.wait_ge(ac_route, 1)
                link(V.tensor_reduce(r_a, r_prob, AX.X, ALU.add))
                link(V.reciprocal(r_b, r_a))
                link(V.tensor_tensor(r_prob, r_prob, bc(r_b, 2, E), ALU.mult))
                for top, one in ((r_p1, r_one), (r_p2, r_two)):
                    link(V.tensor_reduce(top, r_prob, AX.X, ALU.max))
                    link(V.tensor_tensor(r_sel, r_prob, bc(top, 2, E), ALU.is_equal))
                    link(V.tensor_tensor(r_sel, r_sel, rank, ALU.mult))
                    link(V.tensor_reduce(r_a, r_sel, AX.X, ALU.max))
                    link(V.tensor_tensor(one, rank, bc(r_a, 2, E), ALU.is_equal))
                    if one is r_one:
                        link(V.scalar_tensor_tensor(r_prob, one, -2.0, r_prob, ALU.mult, ALU.add))
                link(V.tensor_tensor(r_a, r_p1, r_p2, ALU.add))
                link(V.tensor_scalar(r_a, r_a, EPS_TOP, None, ALU.add))
                link(V.reciprocal(r_b, r_a))
                for k, top in enumerate((r_p1, r_p2)):
                    V.tensor_tensor(pay[:, k, :, 1].bitcast(F32), top, r_b, ALU.mult)
                    V.tensor_copy(pay[:, k, :, 0], token_s[:, 0:TILES])
                link(V.tensor_tensor(masks_b[:], r_one, r_two, ALU.add))
                for e in range(E):
                    i = V.tensor_tensor_scan(r_sum[:, :, e], ones_b[:, 0:TILES], masks_b[:, :, e], 0.0, ALU.mult, ALU.add)
                link(i)
                V.tensor_copy(total_b[:], r_sum[:, TILES - 1, :])
                V.tensor_tensor(before_b[:], r_sum, masks_b[:], ALU.subtract).then_inc(dv_masks, 1)

            def place():
                dv.wait_ge(pe_rank, 1)
                link(V.tensor_tensor(r_pos, ps[:, RANK, 0:TILES * E].rearrange("p (t e) -> p t e", e=E),
                                     bc(expert_s[:, 0, :], 1, TILES), ALU.add))
                for k, one in enumerate((r_one, r_two)):
                    link(V.tensor_tensor(r_sel, r_pos, one, ALU.mult))
                    link(V.tensor_reduce(r_a, r_sel, AX.X, ALU.add))
                    link(V.tensor_copy(pos[:, k, :], r_a))
                link(V.tensor_scalar(counts[0:1, 1, 0:E], ps[0:1, RANK, cut(TILES * E, E)], float(BLK - 1), None, ALU.add))
                link(V.tensor_single_scalar(counts[0:1, 2, 0:E], counts[0:1, 1, 0:E], BLK.bit_length() - 1, ALU.arith_shift_right))
                V.tensor_scalar(counts[0:1, 0, 0:E], counts[0:1, 2, 0:E], 1, None, ALU.max).then_inc(dv_counts, 1)
                V.tensor_copy(r_a[:, 0:1], r_b[:, 0:1]).then_inc(dv_pos, 1)

            block_of(0, None)
            low_weights(1, 1)
            choose()
            block_of(1, end_shared)
            place()
            with dv.Fori(2, NBLK) as g:
                block_of(dv.snap(g, min_val=2, max_val=NBLK - 1), end_shared)

            def begin(e, b, g, was, now):
                block_of(g, end_shared if isinstance(g, int) else end_routed)

            def new_expert(e, par, v):
                if v is None:
                    low_weights(e + 2, 0)
                    dv.wait_ge(b_out, 16 * NBLK)
                elif par == 0:
                    low_weights(e + 2, 1)
                else:
                    with dv.If(v < 2):
                        low_weights(e + 2, 0)
                    dv.nop()

            routed(dv, begin, new_expert, end_routed)


def kernel(**inputs):
    import numpy as np
    import concourse.bacc as bacc
    from concourse.bass_utils import run_bass_kernel_spmd

    def rows_on_partitions(w):
        return w.reshape(-1, P, w.shape[-1]).transpose(1, 0, 2)

    def expert(gate, up, down):
        return np.concatenate([rows_on_partitions(w.T).reshape(P, -1) for w in (gate, up, down)], axis=1)

    i = {k: np.asarray(v) for k, v in inputs.items()}
    experts = [expert(i["L0_ffn_shared_gate"], i["L0_ffn_shared_up"], i["L0_ffn_shared_down"])]
    experts += [expert(i["L0_ffn_routed_gate"][e], i["L0_ffn_routed_up"][e], i["L0_ffn_routed_down"][e]) for e in range(E)]
    row = np.arange(SP_).reshape(CH, P)
    slot = np.arange(E * TOK)
    arrays = {
        "x": i["x"].reshape(TOK, D),
        "ctx_t": i["ctx_768"].reshape(B * M, DC).T,
        "mask": i["mask_BxS2_bf1"].view(np.uint8),
        "mask_t": i["mask_BxS2_bf1"].view(np.uint8).T,
        "wq": rows_on_partitions(i["L0_xattn_Wq"]),
        "wk": i["L0_xattn_Wk"],
        "wv": i["L0_xattn_Wv"],
        "wo": rows_on_partitions(i["L0_xattn_Wo"]),
        "router": rows_on_partitions(i["L0_ffn_router_w"].T),
        "experts": np.stack(experts),
        "ident": np.eye(P, dtype=np.float32),
        "head_sel": (np.arange(P)[:, None] // HD == np.arange(HH)).astype(np.float32),
        "val_sel": np.stack([((row // M - np.array(FIRST_HEAD)[:, None] == j) & (row < SC)).T for j in range(HMAX)],
                            axis=2).astype(np.float32),
        "upper": (np.arange(P)[:, None] < np.arange(P)).astype(np.float32),
        "expert_no": np.broadcast_to(np.stack([np.arange(E) * TOK, E - np.arange(E)]), (P, 2, E)).astype(np.float32),
        "token_no": (np.arange(TILES + 1) * P + np.arange(P)[:, None]).astype(np.int32),
        "pads": np.stack([TOK + slot % P, 0 * slot], axis=1).astype(np.int32),
    }
    nc = bacc.Bacc("TRN2", target_bir_lowering=False, num_devices=1)
    feeds, args = {}, []
    for name, a in arrays.items():
        feeds[f"in_{name}"] = np.ascontiguousarray(a)
        args.append(nc.dram_tensor(f"in_{name}", a.shape, mybir.dt.from_np(a.dtype), kind="ExternalInput").ap())
    args.append(nc.dram_tensor("out_rows", (TOK + P, D), F32, kind="ExternalOutput").ap())
    program(nc, *args)
    result = run_bass_kernel_spmd(nc, [feeds], core_ids=[0])
    return result.results[0]["out_rows"][:TOK].reshape(B, N, D)
```

```python
import concourse.bass as bass
from concourse import mybir
from contextlib import ExitStack

F32 = mybir.dt.float32
F32R = mybir.dt.float32r
I32 = mybir.dt.int32
U8 = mybir.dt.uint8
BF16 = mybir.dt.bfloat16
ACT = mybir.ActivationFunctionType
ALU = mybir.AluOpType
AX = mybir.AxisListType

P = 128
B, N, D = 4, 1024, 256
M, DC = 77, 192
H, HD = 16, 16
F, E = 1024, 7
TOK = B * N
TILES = TOK // P
TPB_LOG = 3
KT = D // P
HH = H // 2
SC = HH * M
CH = -(-SC // P)
SP_ = CH * P
VW = HD + 1
FIRST_HEAD = [c * P // M for c in range(CH)]
HEADS_IN = [min(HH - 1, (c * P + P - 1) // M) - c * P // M + 1 for c in range(CH)]
HMAX = max(HEADS_IN)
BLK = 256
NBLK = TOK // BLK
FT = F // P
WCOLS = 3 * KT * F
EPS_LN = 1e-5
EPS_TOP = 1e-9
UNROLL = 4
LX = 3
PIECE = WCOLS // TILES
WCH = 1024
NW = WCOLS // WCH
GU_CHUNKS = 2 * KT * F // WCH


CONST_LOADS, CTX_LOADS = 9, 8
ROUTE_AT = 3


def cut(o, n):
    return slice(o, o + n)


def bc(ap, axis, n):
    a = ap.unsqueeze(axis)
    return a.to_broadcast([n if k == axis else s for k, s in enumerate(a.shape)])


def program(nc, x, ctx_t, mask, mask_t, wq, wk, wv, wo, router, experts, ident, head_sel, val_sel, upper,
            expert_no, token_no, pads, out):
    xn2_d = nc.dram_tensor("xn2_d", (TOK + P, D), F32, kind="Internal").ap()
    x1_d = nc.dram_tensor("x1_d", (TOK, D), F32, kind="Internal").ap()
    val_d = nc.dram_tensor("val_d", (B, H * M, VW), F32, kind="Internal").ap()
    table_d = nc.dram_tensor("table_d", (E * TOK, 2), I32, kind="Internal").ap()

    with ExitStack() as stack:
        def sb(name, shape, dt=F32):
            return stack.enter_context(nc.sbuf_tensor(name, shape, dt))

        def sem(name):
            return stack.enter_context(nc.semaphore(name))

        def sems(name, n):
            return [sem(f"{name}{k}") for k in range(n)]

        ident_s = sb("ident_s", [P, P])
        wq_s = sb("wq_s", [P, KT, D])
        wo_s = sb("wo_s", [P, KT, D])
        wr_s = sb("wr_s", [P, KT, E])
        keys = sb("keys", [P, B, KT, SC])
        vals = sb("vals", [P, B, KT, CH * HMAX * VW])
        arena = sb("arena", [P, 5 * FT * P])
        taken = {"A": 0, "B": 0}

        def part(phase, *shape):
            n = 1
            for k in shape:
                n *= k
            o = taken[phase]
            taken[phase] = o + n
            assert taken[phase] <= 5 * FT * P
            ap = arena[:, cut(o, n)]
            if len(shape) == 2:
                ap = ap.rearrange("p (a b) -> p a b", a=shape[0])
            return ap

        xa = part("A", UNROLL, D)
        xr = part("A", 2, D)
        xn = part("A", 2, D)
        xnT = part("A", KT, P)
        qT = part("A", KT, P)
        prob = part("A", KT, SP_)
        probT = part("A", KT, SP_)
        xin = part("B", 2, D)
        x1b = part("B", 2, D)
        y = part("B", 2, D)
        gate = part("B", 2, 2 * BLK)
        hid = part("B", FT, BLK)
        mv1 = sb("mv1", [P, 2, 3])
        mv2 = sb("mv2", [P, 2, 3])
        stat1 = sb("stat1", [P, 2, 6])
        stat2 = sb("stat2", [P, 2, 6])
        smax = sb("smax", [P, KT, HH])
        rsum = sb("rsum", [P, H])
        att = sb("att", [P, D])
        attT = sb("attT", [P, KT, P])
        x1 = sb("x1", [P, 2, D])
        xn2 = sb("xn2", [P, 2, D])
        xn2T = sb("xn2T", [P, KT, P])
        logits = sb("logits", [P, TILES, E])
        zero = sb("zero", [P, D])
        power = sb("power", [P, 1])
        upper_s = sb("upper_s", [P, P], BF16)
        ones_b = sb("ones_b", [P, P], BF16)
        masks_b = sb("masks_b", [P, TILES, E], BF16)
        before_b = sb("before_b", [P, TILES, E], BF16)
        total_b = sb("total_b", [P, E], BF16)
        expert_s = sb("expert_s", [P, 2, E])
        token_s = sb("token_s", [P, TILES + 1], I32)
        pay = sb("pay", [P, 2, TILES, 2], I32)
        pos = sb("pos", [P, 2, TILES], I32)
        counts = sb("counts", [1, 3, 8], I32)
        keys_f = keys[:].rearrange("p b k n -> p (b k n)")

        def route_part(k):
            return keys_f[:, cut(k * TILES * E, TILES * E)].rearrange("p (t e) -> p t e", e=E)

        def route_col(k):
            return keys_f[:, cut(6 * TILES * E + k * TILES, TILES)]

        r_prob, r_sel, r_one, r_two, r_sum, r_pos = (route_part(k) for k in range(6))
        r_a, r_p1, r_p2, r_b, r_w = (route_col(k) for k in range(5))
        raw = sb("raw", [P, WCOLS])
        w_hi = [sb(f"w_hi{k}", [P, WCOLS], F32R) for k in range(2)]
        w_lo = [sb(f"w_lo{k}", [P, WCOLS], F32R) for k in range(2)]
        xT_hi = sb("xT_hi", [P, KT, BLK], F32R)
        xT_lo = sb("xT_lo", [P, KT, BLK], F32R)
        hid_hi = sb("hid_hi", [P, FT, BLK], F32R)
        hid_lo = sb("hid_lo", [P, FT, BLK], F32R)
        slots_g = sb("slots_g", [P, 2, 2], I32)
        slots_s = sb("slots_s", [P, 2, 2], I32)
        ps = stack.enter_context(nc.psum_tensor("ps", [P, 8, 512], F32))
        S0, T0, T1, M1, M2 = 0, 4, 5, 6, 7
        XT_BANK, GATE, UP, Y_BANK, RANK = 0, 1, 3, 5, 7

        ctx_s = raw[:, cut(0, 2 * B * M)].rearrange("p (k n) -> p k n", k=2)
        wkv_s = raw[:, cut(1024, 4 * D)].rearrange("p (w k n) -> p w k n", w=2, k=2)
        keys_m, keep, drop, fill = (raw[:, cut(2048 + 320 * k, B * M)] for k in range(4))
        val_x = raw[:, cut(3400, B * H * VW)].rearrange("p (b n) -> p b n", b=B)
        val_c = raw[:, cut(4500, B * KT * CH * VW)].rearrange("p (b k c w) -> p b k c w", b=B, k=KT, c=CH)
        scratch = sb("scratch", [P, 64])
        count, rcount, ksum, kmean, some, none = (scratch[:, cut(4 * k, 4)] for k in range(6))
        keep_k, keep_v = (scratch[:, cut(32 + 4 * k, 4)] for k in range(2))
        mask_s = sb("mask_s", [P, B * M], U8)
        mask_k = sb("mask_k", [P, B], U8)
        head_s = sb("head_s", [P, HH])
        valsel_s = sb("valsel_s", [P, CH, HMAX])
        upper_f = sb("upper_f", [P, P])

        ld_const, ld_ctx, ld_raw0, ld_pads = sem("ld_const"), sem("ld_ctx"), sem("ld_raw0"), sem("ld_pads")
        dv_zero, st_zero, dv_link, pe_keys, pe_vals, dv_keys = (sem(n) for n in ("dv_zero", "st_zero", "dv_link", "pe_keys", "pe_vals", "dv_keys"))
        dv_valx, st_val, ld_valc, dv_vals, po_vc0, po_pad = (sem(n) for n in ("dv_valx", "st_val", "ld_valc", "dv_vals", "po_vc0", "po_pad"))
        ld_xa, ld_xr = sems("ld_xa", UNROLL), sems("ld_xr", 2)
        st_x1, st_xn2 = sems("st_x1", 2), sems("st_xn2", 2)
        dv_bn1, dv_ag1, dv_bn2, dv_ag2 = (sem(n) for n in ("dv_bn1", "dv_ag1", "dv_bn2", "dv_ag2"))
        po_eps1, po_pow1, po_dev1, po_eps2, po_pow2, po_dev2 = (sem(n) for n in ("po_eps1", "po_pow1", "po_dev1", "po_eps2", "po_pow2", "po_dev2"))
        ac_xn, ac_xn2, po_whi, po_wlo = (sem(n) for n in ("ac_xn", "ac_xn2", "po_whi", "po_wlo"))
        pe_xt, pe_qp, pe_ot, pe_wo, pe_x2t, pe_r = (sem(n) for n in ("pe_xt", "pe_qp", "pe_ot", "pe_wo", "pe_x2t", "pe_r"))
        pe_s, pe_eta, pe_etb, pe_pv = (sems(n, 2) for n in ("pe_s", "pe_eta", "pe_etb", "pe_pv"))
        ac_xnt, ac_qt, ac_ont, ac_x2t = (sem(n) for n in ("ac_xnt", "ac_qt", "ac_ont", "ac_x2t"))
        ac_exp, ac_eta = sems("ac_exp", 2), sems("ac_eta", 2)
        dv_max, dv_sub, dv_etb = sems("dv_max", 2), sems("dv_sub", 2), sems("dv_etb", 2)
        dv_rc, dv_norm, dv_x1, dv_l = (sem(n) for n in ("dv_rc", "dv_norm", "dv_x1", "dv_l"))
        dv_shifted, ac_route, dv_masks, pe_rank, dv_pos, dv_counts, st_table = (sem(n) for n in ("dv_shifted", "ac_route", "dv_masks", "pe_rank", "dv_pos", "dv_counts", "st_table"))
        b_xin, b_x1, b_out, b_gather, b_slots_g, b_slots_s, b_add = (sem(n) for n in ("b_xin", "b_x1", "b_out", "b_gather", "b_slots_g", "b_slots_s", "b_add"))
        b_t, b_xhi, b_xlo, b_y, b_ysb = (sem(n) for n in ("b_t", "b_xhi", "b_xlo", "b_y", "b_ysb"))
        b_g, b_u, b_silu, b_h, b_hhi, b_hlo = (sems(n, 4) for n in ("b_g", "b_u", "b_silu", "b_h", "b_hhi", "b_hlo"))
        ld_raw, b_whi, b_wlo = sem("ld_raw"), sem("b_whi"), sem("b_wlo")

        waited = {name: sem(f"{name}_waited") for name in ("DVE", "Pool", "SP")}

        block = stack.enter_context(nc.Block())

        def phase_a(eng, step, first, last, with_batch=False):
            batch = lambda f: [f] if with_batch else []
            lo, hi = UNROLL, TILES - UNROLL
            for i in range(first, lo):
                step(i % UNROLL, lambda o, i=i: 0 <= i + o < TILES, lambda o, i=i: i + o, *batch(lambda o, i=i: (i + o) >> TPB_LOG))
            with eng.Fori(lo // UNROLL, hi // UNROLL) as u:
                t = u * UNROLL
                at = {o: eng.snap(t + o, min_val=lo + o, max_val=hi - UNROLL + o)
                      for o in range(-LX - 1, 2 * UNROLL)}
                if with_batch:
                    of_body = eng.snap(u >> 1, min_val=0, max_val=B - 1)
                    before = eng.snap((t - 1) >> TPB_LOG, min_val=0, max_val=B - 1)
                    batches = {-1: before, **{o: of_body for o in range(UNROLL)}}
                for j in range(UNROLL):
                    step(j, lambda o: True, lambda o, j=j: at[j + o], *batch(lambda o, j=j: batches[j + o]))
            for i in range(hi, last + 1):
                step(i % UNROLL, lambda o, i=i: 0 <= i + o < TILES, lambda o, i=i: i + o, *batch(lambda o, i=i: (i + o) >> TPB_LOG))

        def uses(tile, slot, ring):
            return ((tile - slot) >> (ring.bit_length() - 1)) + 1

        def routed(eng, begin, new_expert, finish):
            g = eng.alloc_register(f"{eng.engine.name}_g")

            def next_block(e, b, was, now, v=None):
                n = eng.snap(g, min_val=NBLK + 1, max_val=(E + 1) * NBLK - 1)
                begin(e, b, n, was, now, v)
                eng.reg_add(g, g, 1)

            def blocks(e, par):
                n = eng.value_load(counts[0:1, 0, bass.ds(e, 1)], min_val=1, max_val=NBLK)
                with eng.Fori(0, 5) as q:
                    with eng.If(q * 3 + 1 < n):
                        with eng.Fori(0, 3) as j:
                            b = eng.snap(q * 3 + j + 1, min_val=1, max_val=NBLK - 1)
                            with eng.If(b < n):
                                next_block(e, b, par, par)
                            eng.nop()
                    eng.nop()

            eng.wait_ge(dv_counts, 1)
            begin(0, 0, NBLK, 0, 1, None)
            eng.reg_mov(g, NBLK + 1)
            if new_expert:
                new_expert(0, 1, None)
            blocks(0, 1)
            with eng.Fori(0, (E - 1) // 2) as v:
                v = eng.snap(v, min_val=0, max_val=(E - 1) // 2 - 1)
                for k in range(2):
                    e = eng.snap(v * 2 + (1 + k), min_val=1 + k, max_val=E - 2 + k)
                    next_block(e, 0, 1 - k, k, v)
                    if new_expert:
                        new_expert(e, k, v)
                    blocks(e, k)
            finish(eng.snap(g, min_val=NBLK + E, max_val=(E + 1) * NBLK))

        def apart(eng):
            eng.sem_inc(waited[eng.engine.name], 1)

        def rows(ap, r, n=2):
            return ap[bass.ds(r, n * P), :].rearrange("(t p) d -> p t d", p=P)

        @block.sync
        def _(sp):
            for dst, src in ((ident_s[:], ident), (wq_s[:], wq), (wo_s[:], wo), (wr_s[:], router),
                             (head_s[:], head_sel), (valsel_s[:], val_sel), (upper_f[:], upper),
                             (expert_s[:], expert_no), (token_s[:], token_no)):
                sp.dma_start(dst, src).then_inc(ld_const, 16)
            for i in range(UNROLL):
                sp.dma_start(xa[:, i, :], x[cut(i * P, P), :]).then_inc(ld_xa[i], 16)
            sp.dma_start(table_d, pads).then_inc(ld_pads, 16)
            sp.wait_ge(dv_zero, 1)
            sp.dma_start(xn2_d[cut(TOK, P), :], zero[:]).then_inc(st_zero, 16)
            sp.dma_start(out[cut(TOK, P), :], zero[:]).then_inc(st_zero, 16)
            sp.wait_ge(dv_valx, 1)
            for b in range(B):
                sp.dma_start(val_d[b].rearrange("(h k) c -> k h c", k=M),
                             val_x[0:M, b, :].rearrange("k (h c) -> k h c", h=H)).then_inc(st_val, 16)
            sp.wait_ge(st_val, 16 * B)
            sp.wait_ge(po_vc0, 1)
            full = (CH - 1) * P
            for b in range(B):
                for h in range(KT):
                    sp.dma_start(val_c[:, b, h, 0:CH - 1, :],
                                 val_d[b, cut(h * SC, full), :].rearrange("(c p) w -> p c w", p=P)).then_inc(ld_valc, 16)
                    sp.dma_start(val_c[0:SC - full, b, h, CH - 1, :],
                                 val_d[b, cut(h * SC + full, SC - full), :]).then_inc(ld_valc, 16)
            sp.wait_ge(dv_vals, 1)
            sp.dma_start(raw[:], experts[0]).then_inc(ld_raw0, 16)

            def step(s, has, tile):
                if has(-2):
                    sp.wait_ge(dv_x1, tile(-2) + 1)
                if has(0):
                    sp.dma_start(xr[:, s % 2, :], x[bass.ds(tile(0) * P, P), :]).then_inc(ld_xr[s % 2], 16)
                if has(-2):
                    sp.dma_start(x1_d[bass.ds(tile(-2) * P, P), :], x1[:, s % 2, :]).then_inc(st_x1[s % 2], 16)
                    sp.wait_ge(ac_xn2, tile(-2) + 1)
                    sp.dma_start(xn2_d[bass.ds(tile(-2) * P, P), :], xn2[:, s % 2, :]).then_inc(st_xn2[s % 2], 16)
                if has(0) and has(UNROLL):
                    sp.wait_ge(ac_xn, tile(0) + 1)
                    sp.dma_start(xa[:, s, :], x[bass.ds(tile(UNROLL) * P, P), :]).then_inc(ld_xa[s], 16)

            phase_a(sp, step, 0, TILES + 1)
            for k in range(2):
                sp.wait_ge(st_x1[k], 16 * (TILES // 2))
                sp.wait_ge(st_xn2[k], 16 * (TILES // 2))
            sp.wait_ge(st_zero, 32)
            sp.dma_start(xin[:], rows(xn2_d, 0)).then_inc(b_xin, 16)
            sp.dma_start(x1b[:], rows(x1_d, 0)).then_inc(b_x1, 16)
            sp.wait_ge(po_wlo, TILES)
            sp.dma_start(raw[:], experts[1]).then_inc(ld_raw, 16)

            sp.wait_ge(b_t, 1)
            sp.dma_start(xin[:], rows(xn2_d, BLK)).then_inc(b_xin, 16)
            with sp.Fori(1, NBLK - 1) as n:
                n = sp.snap(n, min_val=1, max_val=NBLK - 2)
                sp.wait_ge(b_ysb, n)
                sp.dma_start(rows(out, (n - 1) * BLK), y[:]).then_inc(b_out, 16)
                sp.dma_start(x1b[:], rows(x1_d, n * BLK)).then_inc(b_x1, 16)
                sp.wait_ge(b_t, n + 1)
                sp.dma_start(xin[:], rows(xn2_d, (n + 1) * BLK)).then_inc(b_xin, 16)
            sp.wait_ge(b_ysb, NBLK - 1)
            sp.dma_start(rows(out, (NBLK - 2) * BLK), y[:]).then_inc(b_out, 16)
            sp.dma_start(x1b[:], rows(x1_d, (NBLK - 1) * BLK)).then_inc(b_x1, 16)

            last_row = sp.alloc_register("sp_last_row")

            def begin(e, b, g, was, now, v):
                if isinstance(g, int):
                    sp.wait_ge(st_table, 16 * 2 * TILES)
                    sp.dma_start(slots_g[:], rows(table_d, 0)).then_inc(b_slots_g, 16)
                    sp.wait_ge(b_ysb, NBLK)
                    sp.dma_start(rows(out, (NBLK - 1) * BLK), y[:]).then_inc(b_out, 16)
                    sp.reg_mov(last_row, 0)
                    return
                row = sp.snap(e * TOK + b * BLK, min_val=BLK, max_val=E * TOK - BLK)
                sp.wait_ge(b_gather, (g - NBLK) * 32)
                sp.dma_start(slots_g[:], rows(table_d, row)).then_inc(b_slots_g, 16)
                end(g)
                sp.reg_mov(last_row, row)

            def end(g):
                before = sp.snap(last_row, min_val=0, max_val=E * TOK - BLK)
                sp.wait_ge(b_add, (g - NBLK) * 32)
                sp.dma_start(slots_s[:], rows(table_d, before)).then_inc(b_slots_s, 16)

            def finish(g):
                end(g)
                sp.wait_ge(b_out, 16 * NBLK)
                sp.wait_ge(b_add, (g - NBLK) * 32 + 32)
                apart(sp)

            routed(sp, begin, None, finish)

        @block.gpsimd
        def _(po):
            def deviation(mv, s_eps, s_pow, s_dev, n):
                po.tensor_scalar(mv[:, 1:2], mv[:, 1:2], EPS_LN, None, ALU.add).then_inc(s_eps, 1)
                po.wait_ge(s_eps, n)
                po.tensor_tensor(mv[:, 1:2], mv[:, 1:2], power[:], ALU.pow).then_inc(s_pow, 1)
                po.wait_ge(s_pow, n)
                apart(po)
                po.tensor_scalar(mv[:, 2:3], mv[:, 0:1], mv[:, 1:2], -1.0, ALU.mult, ALU.mult).then_inc(s_dev, 1)

            po.memset(prob[:, :, SC:], 0.0).then_inc(po_pad, 1)
            po.memset(val_c, 0.0).then_inc(po_vc0, 1)
            po.wait_ge(dv_zero, 1)

            def step(s, has, tile):
                if has(-2):
                    po.wait_ge(dv_ag2, tile(-2) + 1)
                    apart(po)
                    deviation(mv2[:, s % 2, :], po_eps2, po_pow2, po_dev2, tile(-2) + 1)
                if has(2):
                    po.wait_ge(dv_ag1, tile(2) + 1)
                    apart(po)
                    deviation(mv1[:, s % 2, :], po_eps1, po_pow1, po_dev1, tile(2) + 1)
                if has(-2):
                    o = tile(-2) * PIECE
                    if isinstance(o, int) and o == 0:
                        po.wait_ge(ld_raw0, 16)
                    po.tensor_copy(w_hi[0][:, bass.ds(o, PIECE)], raw[:, bass.ds(o, PIECE)]).then_inc(po_whi, 1)
                    po.wait_ge(po_whi, tile(-2) + 1)
                    po.tensor_tensor(w_lo[0][:, bass.ds(o, PIECE)], raw[:, bass.ds(o, PIECE)],
                                     w_hi[0][:, bass.ds(o, PIECE)].bitcast(F32), ALU.subtract).then_inc(po_wlo, 1)

            phase_a(po, step, -2, TILES + 1)

            po.wait_ge(dv_pos, 1)
            po.wait_ge(ld_pads, 16)
            for t in range(TILES):
                for k in range(2):
                    po.indirect_dma_start(out=table_d, out_offset=bass.IndirectOffsetOnAxis(ap=pos[:, k, t:t + 1], axis=0),
                                          in_=pay[:, k, t, :], in_offset=None).then_inc(st_table, 16)

            def begin(e, b, g, was, now, v):
                r = g - NBLK
                po.wait_ge(b_slots_g, r * 16 + 16)
                po.wait_ge(b_t, g)
                apart(po)
                for t in range(2):
                    po.indirect_dma_start(out=xin[:, t, :], out_offset=None, in_=xn2_d,
                                          in_offset=bass.IndirectOffsetOnAxis(ap=slots_g[:, t, 0:1], axis=0)).then_inc(b_gather, 16)
                if not isinstance(g, int):
                    add(g)

            def add(g):
                r = g - NBLK
                po.wait_ge(b_ysb, g)
                for t in range(2):
                    po.wait_ge(b_add, r * 32 + 16 * t)
                    apart(po)
                    po.indirect_dma_start(out=out, out_offset=bass.IndirectOffsetOnAxis(ap=slots_s[:, t, 0:1], axis=0),
                                          in_=y[:, t, :], in_offset=None, compute_op=ALU.add).then_inc(b_add, 16)

            def first_expert(e, par, v):
                if v is None:
                    po.wait_ge(b_out, 16 * NBLK)
                    po.wait_ge(st_zero, 32)
                    for t in range(2):
                        if t:
                            po.wait_ge(b_add, 16)
                        po.indirect_dma_start(out=out, out_offset=bass.IndirectOffsetOnAxis(ap=token_s[:, TILES:TILES + 1], axis=0),
                                              in_=zero[:], in_offset=None, compute_op=ALU.add).then_inc(b_add, 16)

            routed(po, begin, first_expert, add)

        @block.tensor
        def _(pe):
            mm = nc.tensor.matmul

            pe.wait_ge(ld_ctx, 16 * CTX_LOADS)
            for h in range(KT):
                for k, kp in ((0, P), (1, DC - P)):
                    last = mm(ps[:, h, 0:B * M], wkv_s[0:kp, 0, k, cut(h * P, P)], ctx_s[0:kp, k, :],
                              start=k == 0, stop=k == 1)
            last.then_inc(pe_keys, 1)
            for b in range(B):
                for k, kp in ((0, P), (1, DC - P)):
                    last = mm(ps[0:M, 2 + b, 0:D], ctx_s[0:kp, k, cut(b * M, M)], wkv_s[0:kp, 1, k, :],
                              start=k == 0, stop=k == 1)
            last.then_inc(pe_vals, 1)
            pe.wait_ge(ld_const, 16 * CONST_LOADS)
            pe.wait_ge(po_pad, 1)

            def transpose_probs(half):
                for c in range(CH):
                    bank, col = (T0, c * P) if c < 3 else (T1, (c - 3) * P)
                    i = nc.tensor.transpose(ps[:, bank, cut(col, P)], prob[:, half, cut(c * P, P)], ident_s[:])
                    if c == 2:
                        i.then_inc(pe_eta[half], 1)
                i.then_inc(pe_etb[half], 1)

            def attend(half, batch):
                for c in range(CH):
                    n = HEADS_IN[c] * VW
                    i = mm(ps[:, M2, cut((half * HH + FIRST_HEAD[c]) * VW, n)], probT[:, half, cut(c * P, P)],
                           vals[:, batch, half, cut(c * HMAX * VW, n)] if isinstance(batch, int) else
                           vals[:, bass.ds(batch, 1), half, cut(c * HMAX * VW, n)],
                           start=half == 0 and c == 0, stop=half == 1 and c == CH - 1, skip_group_check=True)
                i.then_inc(pe_pv[half], 1)

            def score(half, batch):
                for q in range(2):
                    n = SC // 2
                    i = mm(ps[:, S0 + 2 * half + q, 0:n], qT[:, half, :],
                           keys[:, batch, half, cut(q * n, n)] if isinstance(batch, int) else
                           keys[:, bass.ds(batch, 1), half, cut(q * n, n)], start=True, stop=True)
                i.then_inc(pe_s[half], 1)

            def transpose_rows(dst, src):
                for k in range(KT):
                    i = nc.tensor.transpose(dst[:, cut(k * P, P)], src[:, cut(k * P, P)], ident_s[:])
                return i

            def step(s, has, tile, batch):
                if has(-1):
                    before = batch(-1)
                    pe.wait_ge(ac_exp[1], tile(-1) + 1)
                    pe.wait_ge(ac_eta[0], tile(-1) + 1)
                    pe.wait_ge(dv_etb[0], tile(-1) + 1)
                    transpose_probs(1)
                if has(-LX):
                    pe.wait_ge(ac_xn2, tile(-LX) + 1)
                    if has(0):
                        pe.wait_ge(ac_qt, tile(0) + 1)
                    transpose_rows(ps[:, M1, 0:D], xn2[:, (s - LX) % 2, :]).then_inc(pe_x2t, 1)
                if has(-1):
                    if has(-2):
                        pe.wait_ge(dv_x1, tile(-2) + 1)
                    if has(-LX - 1):
                        pe.wait_ge(dv_l, tile(-LX - 1) + 1)
                    if isinstance(before, int) and tile(-1) == 0:
                        pe.wait_ge(dv_vals, 1)
                    attend(0, before)
                if has(0):
                    now = batch(0)
                    pe.wait_ge(ac_qt, tile(0) + 1)
                    if isinstance(now, int) and tile(0) == 0:
                        pe.wait_ge(dv_keys, 1)
                        pe.wait_ge(dv_valx, 1)
                    score(0, now)
                if has(-1):
                    pe.wait_ge(ac_eta[1], tile(-1) + 1)
                    pe.wait_ge(dv_etb[1], tile(-1) + 1)
                    attend(1, before)
                if has(1):
                    pe.wait_ge(ac_xn, tile(1) + 1)
                    if has(-LX):
                        pe.wait_ge(ac_x2t, tile(-LX) + 1)
                    transpose_rows(ps[:, M1, 0:D], xn[:, (s + 1) % 2, :]).then_inc(pe_xt, 1)
                if has(0):
                    score(1, now)
                if has(1):
                    pe.wait_ge(ac_xnt, tile(1) + 1)
                    for h in range(KT):
                        for k in range(KT):
                            last = mm(ps[:, M1, cut(D + h * P, P)], wq_s[:, k, cut(h * P, P)], xnT[:, k, :],
                                      start=k == 0, stop=k == KT - 1)
                    last.then_inc(pe_qp, 1)
                if has(-1):
                    pe.wait_ge(dv_norm, tile(-1) + 1)
                    transpose_rows(ps[:, T1, D:2 * D], att[:]).then_inc(pe_ot, 1)
                if has(0):
                    pe.wait_ge(ac_exp[0], tile(0) + 1)
                    if has(-1):
                        pe.wait_ge(ac_ont, tile(-1) + 1)
                    transpose_probs(0)
                if has(-1):
                    pe.wait_ge(ac_ont, tile(-1) + 1)
                    for k in range(KT):
                        last = mm(ps[:, M2, 0:D], attT[:, k, :], wo_s[:, k, :], start=k == 0, stop=k == KT - 1)
                    last.then_inc(pe_wo, 1)
                if has(-LX):
                    pe.wait_ge(ac_x2t, tile(-LX) + 1)
                    if not has(-1):
                        if has(-LX - 1):
                            pe.wait_ge(dv_l, tile(-LX - 1) + 1)
                            pe.wait_ge(dv_x1, tile(-2) + 1 if has(-2) else TILES)
                    for k in range(KT):
                        last = mm(ps[:, M2, cut(2 * D - 8, E)], xn2T[:, k, :], wr_s[:, k, :],
                                  start=k == 0, stop=k == KT - 1)
                    last.then_inc(pe_r, 1)

            phase_a(pe, step, -1, TILES + LX - 1, with_batch=True)

            def transpose_block(g, wait):
                wait()
                if not (isinstance(g, int) and g == 0):
                    pe.wait_ge(b_xlo, g)
                for k in range(KT):
                    for t in range(2):
                        i = nc.tensor.transpose(ps[:, XT_BANK, cut(k * BLK + t * P, P)], xin[:, t, cut(k * P, P)], ident_s[:])
                i.then_inc(b_t, 1)

            def down(g, par):
                if not (isinstance(g, int) and g == 1):
                    pe.wait_ge(b_ysb, g - 1)
                for p in range(4):
                    pe.wait_ge(b_hhi[p], g)
                    pe.wait_ge(b_hlo[p], g)
                    for t in range(2):
                        for f in (2 * p, 2 * p + 1):
                            o = 2 * KT * F + f * D
                            for n, (a, w) in enumerate(((hid_hi, w_hi), (hid_lo, w_hi), (hid_hi, w_lo))):
                                i = mm(ps[:, Y_BANK + t, 0:D], a[:, f, cut(t * P, P)], w[par][:, cut(o, D)],
                                       start=f == 0 and n == 0, stop=f == FT - 1 and n == 2)
                i.then_inc(b_y, 1)

            def gate_up(g, par):
                pe.wait_ge(b_xlo, g + 1)
                for p in range(4):
                    if p >= 2:
                        pe.wait_ge(b_h[p - 2], g + 1)
                    for m, (bank, ready) in enumerate(((GATE + p % 2, b_g[p]), (UP + p % 2, b_u[p]))):
                        for f in range(2):
                            for k in range(KT):
                                o = (m * KT + k) * F + (2 * p + f) * P
                                for n, (w, a) in enumerate(((w_hi, xT_hi), (w_hi, xT_lo), (w_lo, xT_hi))):
                                    i = mm(ps[:, bank, cut(f * BLK, BLK)], w[par][:, cut(o, P)], a[:, k, :],
                                           start=k == 0 and n == 0, stop=k == KT - 1 and n == 2)
                        i.then_inc(ready, 1)

            def shared(g):
                transpose_block(g, lambda: pe.wait_ge(b_xin, g * 16 + 16))
                if not (isinstance(g, int) and g == 0):
                    down(g, 0)
                gate_up(g, 0)

            pe.wait_ge(po_wlo, TILES)
            for g in range(ROUTE_AT):
                shared(g)
            pe.wait_ge(dv_masks, 1)
            mm(ps[:, RANK, 0:TILES * E], upper_s[:], masks_b[:].rearrange("p t e -> p (t e)"), start=True, stop=False)
            mm(ps[:, RANK, 0:TILES * E], ones_b[:], before_b[:].rearrange("p t e -> p (t e)"), start=False, stop=True)
            mm(ps[:, RANK, cut(TILES * E, E)], ones_b[:], total_b[:], start=True, stop=True).then_inc(pe_rank, 1)
            shared(ROUTE_AT)
            with pe.Fori(ROUTE_AT + 1, NBLK) as g:
                shared(pe.snap(g, min_val=ROUTE_AT + 1, max_val=NBLK - 1))

            def begin(e, b, g, was, now, v):
                transpose_block(g, lambda: pe.wait_ge(b_gather, (g - NBLK) * 32 + 32))
                down(g, was)
                if isinstance(b, int):
                    pe.wait_ge(b_wlo, (e + 1) * NW)
                gate_up(g, now)

            routed(pe, begin, None, lambda g: down(g, 1))

        @block.scalar
        def _(ac):
            for dst, src in ((ctx_s[:, 0, :], ctx_t[0:P, :]), (ctx_s[0:DC - P, 1, :], ctx_t[P:DC, :]),
                             (wkv_s[:, 0, 0, :], wk[0:P, :]), (wkv_s[0:DC - P, 0, 1, :], wk[P:DC, :]),
                             (wkv_s[:, 1, 0, :], wv[0:P, :]), (wkv_s[0:DC - P, 1, 1, :], wv[P:DC, :]),
                             (mask_s[:], mask.rearrange("b k -> (b k)").unsqueeze(0).partition_broadcast(P)),
                             (mask_k[0:M, :], mask_t)):
                ac.dma_start(dst, src).then_inc(ld_ctx, 16)

            def copy(dst, src):
                return nc.scalar.activation(dst, src, ACT.Copy)

            def soften(half, n):
                ac.wait_ge(dv_sub[half], n)
                nc.scalar.activation(prob[:, half, 0:SC], prob[:, half, 0:SC], ACT.Exp, scale=HD ** -0.5).then_inc(ac_exp[half], 1)

            def probs_a(half, n):
                ac.wait_ge(pe_eta[half], n)
                copy(probT[:, half, 0:3 * P], ps[:, T0, 0:3 * P]).then_inc(ac_eta[half], 1)

            def normalise(dst, src, mv):
                return nc.scalar.activation(dst, src, ACT.Identity, bias=mv[:, 2:3], scale=mv[:, 1:2])

            def step(s, has, tile):
                if has(-1):
                    probs_a(1, tile(-1) + 1)
                if has(-LX):
                    ac.wait_ge(pe_x2t, tile(-LX) + 1)
                    copy(xn2T[:].rearrange("p k n -> p (k n)"), ps[:, M1, 0:D]).then_inc(ac_x2t, 1)
                if has(1):
                    ac.wait_ge(pe_xt, tile(1) + 1)
                    copy(xnT[:].rearrange("p k n -> p (k n)"), ps[:, M1, 0:D]).then_inc(ac_xnt, 1)
                if has(0):
                    soften(0, tile(0) + 1)
                if has(1):
                    ac.wait_ge(pe_qp, tile(1) + 1)
                    copy(qT[:].rearrange("p k n -> p (k n)"), ps[:, M1, D:2 * D]).then_inc(ac_qt, 1)
                if has(-1):
                    ac.wait_ge(pe_ot, tile(-1) + 1)
                    copy(attT[:].rearrange("p k n -> p (k n)"), ps[:, T1, D:2 * D]).then_inc(ac_ont, 1)
                if has(-2):
                    ac.wait_ge(po_dev2, tile(-2) + 1)
                    if has(-4):
                        ac.wait_ge(pe_x2t, tile(-4) + 1)
                        ac.wait_ge(st_xn2[s % 2], uses(tile(-4), s % 2, 2) * 16)
                    normalise(xn2[:, s % 2, :], x1[:, s % 2, :], mv2[:, s % 2, :]).then_inc(ac_xn2, 1)
                if has(0):
                    soften(1, tile(0) + 1)
                    probs_a(0, tile(0) + 1)
                if has(2):
                    ac.wait_ge(po_dev1, tile(2) + 1)
                    if has(0):
                        ac.wait_ge(pe_xt, tile(0) + 1)
                    normalise(xn[:, s % 2, :], xa[:, (s + 2) % UNROLL, :], mv1[:, s % 2, :]).then_inc(ac_xn, 1)

            phase_a(ac, step, -2, TILES + LX - 1)

            def act_block(g, early=None, late=None):
                ac.wait_ge(b_t, g + 1)
                copy(xT_hi[:].rearrange("p k n -> p (k n)"), ps[:, XT_BANK, :]).then_inc(b_xhi, 1)
                if early:
                    early()

                def high(p):
                    ac.wait_ge(b_h[p], g + 1)
                    copy(hid_hi[:, cut(2 * p, 2), :], hid[:, cut(2 * p, 2), :]).then_inc(b_hhi[p], 1)

                for p in range(4):
                    ac.wait_ge(b_g[p], g + 1)
                    if p >= 2:
                        ac.wait_ge(b_h[p - 2], g + 1)
                    nc.scalar.activation(gate[:, p % 2, :], ps[:, GATE + p % 2, :], ACT.Silu).then_inc(b_silu[p], 1)
                    if p:
                        high(p - 1)
                    if late:
                        late(p)
                high(3)

            def high_weights(par, chunks):
                for c in chunks:
                    copy(w_hi[par][:, cut(c * WCH, WCH)], raw[:, cut(c * WCH, WCH)]).then_inc(b_whi, 1)

            def load_raw(at):
                ac.wait_ge(b_wlo, (at - 1) * NW)
                if not isinstance(at, int):
                    at = nc.s_assert_within(at, 0, E, skip_runtime_bounds_check_because="the last body's load is left out")
                ac.dma_start(raw[:], experts[bass.ds(at, 1)].rearrange("a p n -> p (a n)")).then_inc(ld_raw, 16)

            def soften_routes(p):
                if p == 0:
                    ac.wait_ge(dv_shifted, 1)
                    nc.scalar.activation(r_prob, r_prob, ACT.Exp).then_inc(ac_route, 1)

            def first_weights():
                ac.wait_ge(ld_raw, 16)
                high_weights(1, range(NW))

            act_block(0, late=soften_routes)
            act_block(1)
            act_block(2, early=first_weights)
            load_raw(2)
            with ac.Fori(ROUTE_AT, NBLK) as g:
                act_block(ac.snap(g, min_val=ROUTE_AT, max_val=NBLK - 1))

            def begin(e, b, g, was, now, v):
                if not (isinstance(b, int) and b == 0):
                    return act_block(g)
                unless_last = v is not None and now == 1

                def guarded(part):
                    if unless_last:
                        with ac.If(v < (E - 1) // 2 - 1):
                            part()
                        ac.nop()
                    else:
                        part()

                def early():
                    ac.wait_ge(ld_raw, (e + 2) * 16)
                    ac.wait_ge(b_u[3], g)
                    high_weights(was, range(GU_CHUNKS))

                def late(p):
                    if p == 1:
                        def part():
                            ac.wait_ge(b_y, g)
                            high_weights(was, range(GU_CHUNKS, NW))
                        guarded(part)

                act_block(g, early=lambda: guarded(early), late=late)
                if v is None:
                    load_raw(e + 3)
                else:
                    with ac.If(v < (E - 1) // 2 - 1):
                        load_raw(e + 3)
                    ac.nop()

            routed(ac, begin, None, lambda g: None)

        @block.vector
        def _(dv):
            V = nc.vector
            links = [0]

            def link(i):
                links[0] += 1
                i.then_inc(dv_link, 1)
                dv.wait_ge(dv_link, links[0])

            V.memset(power[:], -0.5)
            V.memset(zero[:], 0.0).then_inc(dv_zero, 1)
            V.memset(ones_b[:], 1.0)
            dv.wait_ge(ld_const, 16 * CONST_LOADS)
            V.tensor_copy(upper_s[:], upper_f[:])

            def key_values():
                dv.wait_ge(ld_ctx, 16 * CTX_LOADS)
                V.tensor_copy(keep_k[0:M], mask_k[0:M])
                link(V.tensor_copy(keep, mask_s[:]))
                V.tensor_scalar(drop, keep, -1.0, 1.0, ALU.mult, ALU.add)
                link(V.tensor_reduce(count, keep.rearrange("p (b k) -> p b k", b=B), AX.X, ALU.add))
                V.tensor_scalar(some, count, 1.0, None, ALU.min)
                link(V.tensor_scalar(count, count, 1.0, None, ALU.max))
                V.reciprocal(rcount, count)
                link(V.tensor_scalar(none, some, -1.0, 1.0, ALU.mult, ALU.add))
                link(V.tensor_tensor(keep_v[0:M], keep_k[0:M], none[0:M], ALU.max))
                dv.wait_ge(pe_keys, 1)
                for h in range(KT):
                    link(V.tensor_tensor(keys_m, ps[:, h, 0:B * M], keep, ALU.mult))
                    per_batch = keys_m.rearrange("p (b k) -> p b k", b=B)
                    link(V.tensor_reduce(ksum, per_batch, AX.X, ALU.add))
                    link(V.tensor_tensor(kmean, ksum, rcount, ALU.mult))
                    link(V.tensor_tensor(fill.rearrange("p (b k) -> p b k", b=B), drop.rearrange("p (b k) -> p b k", b=B),
                                         bc(kmean, 2, M), ALU.mult))
                    link(V.tensor_tensor(keys_m, keys_m, fill, ALU.add))
                    for b in range(B):
                        i = V.tensor_tensor(keys[:, b, h, :].rearrange("p (h k) -> p h k", h=HH),
                                            bc(keys_m[:, cut(b * M, M)], 1, HH), bc(head_s[:], 2, M), ALU.mult)
                    link(i)
                V.tensor_copy(scratch[:, 63:64], kmean[:, 0:1]).then_inc(dv_keys, 1)
                dv.wait_ge(pe_vals, 1)
                for b in range(B):
                    by_head = val_x[0:M, b, :].rearrange("k (h c) -> k h c", h=H)
                    V.tensor_scalar(by_head[:, :, 0:HD], ps[0:M, 2 + b, 0:D].rearrange("k (h c) -> k h c", h=H),
                                    keep_v[0:M, b:b + 1], None, ALU.mult)
                    i = V.tensor_copy(by_head[:, :, HD], keep_v[0:M, b:b + 1].to_broadcast([M, H]))
                i.then_inc(dv_valx, 1)

            def chunk_values():
                dv.wait_ge(ld_valc, 16 * B * KT * 2)
                for b in range(B):
                    for h in range(KT):
                        i = V.tensor_tensor(vals[:, b, h, :].rearrange("p (c j w) -> p c j w", c=CH, j=HMAX),
                                            bc(val_c[:, b, h], 2, HMAX), bc(valsel_s[:], 3, VW), ALU.mult)
                i.then_inc(dv_vals, 1)

            def norm_stats(src, stat, mv, s_bn, s_ag, n):
                V.bn_stats(stat, src).then_inc(s_bn, 1)
                dv.wait_ge(s_bn, n)
                apart(dv)
                V.bn_aggr(mv[:, 0:2], stat).then_inc(s_ag, 1)

            def shift(half, n):
                scores = ps[:, cut(S0 + 2 * half, 2), 0:SC // 2].rearrange("p q (h k) -> p q h k", k=M)
                top = smax[:, half, :].rearrange("p (q h) -> p q h", q=2)
                dv.wait_ge(pe_s[half], n)
                V.tensor_reduce(top, scores, AX.X, ALU.max).then_inc(dv_max[half], 1)
                dv.wait_ge(dv_max[half], n)
                V.tensor_tensor(prob[:, half, 0:SC].rearrange("p (q h k) -> p q h k", q=2, k=M), scores,
                                bc(top, 3, M), ALU.subtract).then_inc(dv_sub[half], 1)

            def probs_b(half, n):
                dv.wait_ge(pe_etb[half], n)
                V.tensor_copy(probT[:, half, 3 * P:], ps[:, T1, 0:2 * P]).then_inc(dv_etb[half], 1)

            def step(s, has, tile):
                if has(-2):
                    n = tile(-2) + 1
                    dv.wait_ge(ld_xr[s % 2], uses(tile(-2), s % 2, 2) * 16)
                    if has(-4):
                        dv.wait_ge(st_x1[s % 2], uses(tile(-4), s % 2, 2) * 16)
                        dv.wait_ge(ac_xn2, tile(-4) + 1)
                    dv.wait_ge(pe_wo, n)
                    if has(-LX - 1):
                        dv.wait_ge(pe_r, tile(-LX - 1) + 1)
                    V.tensor_tensor(x1[:, s % 2, :], ps[:, M2, 0:D], xr[:, s % 2, :], ALU.add).then_inc(dv_x1, 1)
                if has(-LX - 1):
                    if not has(-2):
                        dv.wait_ge(pe_r, tile(-LX - 1) + 1)
                    V.tensor_copy(logits[:, bass.ds(tile(-LX - 1), 1), :].rearrange("p a e -> p (a e)"),
                                  ps[:, M2, cut(2 * D - 8, E)]).then_inc(dv_l, 1)
                if has(-2):
                    dv.wait_ge(dv_x1, n)
                    norm_stats(x1[:, s % 2, :], stat2[:, s % 2, :], mv2[:, s % 2, :], dv_bn2, dv_ag2, n)
                if has(-1):
                    probs_b(1, tile(-1) + 1)
                if has(0):
                    shift(0, tile(0) + 1)
                if has(-1):
                    heads = ps[:, M2, 0:H * VW].rearrange("p (h c) -> p h c", h=H)
                    dv.wait_ge(pe_pv[1], tile(-1) + 1)
                    V.reciprocal(rsum[:], heads[:, :, HD]).then_inc(dv_rc, 1)
                    dv.wait_ge(dv_rc, tile(-1) + 1)
                    V.tensor_tensor(att[:].rearrange("p (h c) -> p h c", h=H), heads[:, :, 0:HD],
                                    bc(rsum[:], 2, HD), ALU.mult).then_inc(dv_norm, 1)
                if has(2):
                    n = tile(2) + 1
                    dv.wait_ge(ld_xa[(s + 2) % UNROLL], uses(tile(2), (s + 2) % UNROLL, UNROLL) * 16)
                    if has(0):
                        dv.wait_ge(ac_xn, tile(0) + 1)
                    norm_stats(xa[:, (s + 2) % UNROLL, :], stat1[:, s % 2, :], mv1[:, s % 2, :], dv_bn1, dv_ag1, n)
                if has(0):
                    shift(1, tile(0) + 1)
                    probs_b(0, tile(0) + 1)

            for i in (-2, -1):
                step(i % UNROLL, lambda o, i=i: 0 <= i + o < TILES, lambda o, i=i: i + o)
            key_values()
            chunk_values()
            phase_a(dv, step, 0, TILES + LX)

            def block_of(g, finish, early=None, late=None):
                dv.wait_ge(b_xhi, g + 1)
                V.tensor_tensor(xT_lo[:].rearrange("p k n -> p (k n)"), ps[:, XT_BANK, :],
                                xT_hi[:].rearrange("p k n -> p (k n)").bitcast(F32), ALU.subtract).then_inc(b_xlo, 1)
                if early:
                    early()
                if finish:
                    finish(g)

                def low(p):
                    dv.wait_ge(b_hhi[p], g + 1)
                    pair = cut(2 * p, 2)
                    V.tensor_tensor(hid_lo[:, pair, :], hid[:, pair, :], hid_hi[:, pair, :].bitcast(F32),
                                    ALU.subtract).then_inc(b_hlo[p], 1)

                for p in range(4):
                    dv.wait_ge(b_silu[p], g + 1)
                    dv.wait_ge(b_u[p], g + 1)
                    V.tensor_tensor(hid[:, cut(2 * p, 2), :].rearrange("p f n -> p (f n)"), gate[:, p % 2, :],
                                    ps[:, UP + p % 2, :], ALU.mult).then_inc(b_h[p], 1)
                    if p:
                        low(p - 1)
                    if late:
                        late(p)
                low(3)

            def end_shared(g):
                dv.wait_ge(b_y, g)
                dv.wait_ge(b_x1, g * 16)
                if not (isinstance(g, int) and g == 1):
                    dv.wait_ge(b_out, g * 16 - 16)
                V.tensor_tensor(y, ps[:, cut(Y_BANK, 2), 0:D], x1b, ALU.add).then_inc(b_ysb, 1)

            def end_routed(g):
                dv.wait_ge(b_y, g)
                dv.wait_ge(b_slots_s, (g - NBLK) * 16)
                dv.wait_ge(b_add, (g - NBLK) * 32)
                for t in range(2):
                    i = V.tensor_scalar(y[:, t, :], ps[:, Y_BANK + t, 0:D], slots_s[:, t, 1:2].bitcast(F32), None, ALU.mult)
                i.then_inc(b_ysb, 1)

            def low_weights(at, par, chunks):
                for c in chunks:
                    dv.wait_ge(b_whi, (at - 1) * NW + c + 1)
                    V.tensor_tensor(w_lo[par][:, cut(c * WCH, WCH)], raw[:, cut(c * WCH, WCH)],
                                    w_hi[par][:, cut(c * WCH, WCH)].bitcast(F32), ALU.subtract).then_inc(b_wlo, 1)

            rank = bc(expert_s[:, 1, :], 1, TILES)

            def best(top, one):
                link(V.tensor_reduce(top, r_prob, AX.X, ALU.max))
                link(V.tensor_tensor(r_sel, r_prob, bc(top, 2, E), ALU.is_equal))
                link(V.tensor_tensor(r_sel, r_sel, rank, ALU.mult))
                link(V.tensor_reduce(r_a, r_sel, AX.X, ALU.max))
                link(V.tensor_tensor(one, rank, bc(r_a, 2, E), ALU.is_equal))

            def choose_first(p):
                if p == 0:
                    link(V.tensor_reduce(r_a, logits[:], AX.X, ALU.max))
                    V.tensor_tensor(r_prob, logits[:], bc(r_a, 2, E), ALU.subtract).then_inc(dv_shifted, 1)
                if p == 2:
                    dv.wait_ge(ac_route, 1)
                    link(V.tensor_reduce(r_a, r_prob, AX.X, ALU.add))
                    link(V.reciprocal(r_b, r_a))
                    link(V.tensor_tensor(r_prob, r_prob, bc(r_b, 2, E), ALU.mult))
                if p == 3:
                    best(r_p1, r_one)

            def choose_second(p):
                if p == 0:
                    link(V.scalar_tensor_tensor(r_prob, r_one, -2.0, r_prob, ALU.mult, ALU.add))
                    best(r_p2, r_two)
                if p == 1:
                    link(V.tensor_tensor(r_a, r_p1, r_p2, ALU.add))
                    link(V.tensor_scalar(r_a, r_a, EPS_TOP, None, ALU.add))
                    link(V.reciprocal(r_b, r_a))
                    for k, top in enumerate((r_p1, r_p2)):
                        V.tensor_tensor(pay[:, k, :, 1].bitcast(F32), top, r_b, ALU.mult)
                        V.tensor_copy(pay[:, k, :, 0], token_s[:, 0:TILES])
                    link(V.tensor_tensor(masks_b[:], r_one, r_two, ALU.add))
                if p == 2:
                    for e in range(E):
                        i = V.tensor_tensor_scan(r_sum[:, :, e], ones_b[:, 0:TILES], masks_b[:, :, e], 0.0, ALU.mult, ALU.add)
                    link(i)
                    V.tensor_copy(total_b[:], r_sum[:, TILES - 1, :])
                    V.tensor_tensor(before_b[:], r_sum, masks_b[:], ALU.subtract).then_inc(dv_masks, 1)

            def place():
                dv.wait_ge(pe_rank, 1)
                link(V.tensor_tensor(r_pos, ps[:, RANK, 0:TILES * E].rearrange("p (t e) -> p t e", e=E),
                                     bc(expert_s[:, 0, :], 1, TILES), ALU.add))
                for k, one in enumerate((r_one, r_two)):
                    link(V.tensor_tensor(r_sel, r_pos, one, ALU.mult))
                    link(V.tensor_reduce(r_a, r_sel, AX.X, ALU.add))
                    link(V.tensor_copy(pos[:, k, :], r_a))
                link(V.tensor_scalar(counts[0:1, 1, 0:E], ps[0:1, RANK, cut(TILES * E, E)], float(BLK - 1), None, ALU.add))
                link(V.tensor_single_scalar(counts[0:1, 2, 0:E], counts[0:1, 1, 0:E], BLK.bit_length() - 1, ALU.arith_shift_right))
                V.tensor_scalar(counts[0:1, 0, 0:E], counts[0:1, 2, 0:E], 1, None, ALU.max).then_inc(dv_counts, 1)
                V.tensor_copy(r_a[:, 0:1], r_b[:, 0:1]).then_inc(dv_pos, 1)

            block_of(0, None, late=choose_first)
            block_of(1, end_shared, late=choose_second)
            block_of(2, end_shared, early=lambda: low_weights(1, 1, range(GU_CHUNKS)),
                     late=lambda p: low_weights(1, 1, range(GU_CHUNKS, NW)) if p == 1 else None)
            block_of(ROUTE_AT, end_shared, early=place)
            with dv.Fori(ROUTE_AT + 1, NBLK) as g:
                block_of(dv.snap(g, min_val=ROUTE_AT + 1, max_val=NBLK - 1), end_shared)

            def begin(e, b, g, was, now, v):
                finish = end_shared if isinstance(g, int) else end_routed
                if not (isinstance(b, int) and b == 0):
                    return block_of(g, finish)
                unless_last = v is not None and now == 1

                def guarded(part):
                    if unless_last:
                        with dv.If(v < (E - 1) // 2 - 1):
                            part()
                        dv.nop()
                    else:
                        part()

                def late(p):
                    if p == 1:
                        guarded(lambda: low_weights(e + 2, was, range(GU_CHUNKS, NW)))

                block_of(g, finish, early=lambda: guarded(lambda: low_weights(e + 2, was, range(GU_CHUNKS))), late=late)

            def new_expert(e, par, v):
                if v is None:
                    dv.wait_ge(b_out, 16 * NBLK)

            routed(dv, begin, new_expert, end_routed)


def kernel(**inputs):
    import numpy as np
    import concourse.bacc as bacc
    from concourse.bass_utils import run_bass_kernel_spmd

    def rows_on_partitions(w):
        return w.reshape(-1, P, w.shape[-1]).transpose(1, 0, 2)

    def expert(gate, up, down):
        return np.concatenate([rows_on_partitions(w.T).reshape(P, -1) for w in (gate, up, down)], axis=1)

    i = {k: np.asarray(v) for k, v in inputs.items()}
    experts = [expert(i["L0_ffn_shared_gate"], i["L0_ffn_shared_up"], i["L0_ffn_shared_down"])]
    experts += [expert(i["L0_ffn_routed_gate"][e], i["L0_ffn_routed_up"][e], i["L0_ffn_routed_down"][e]) for e in range(E)]
    row = np.arange(SP_).reshape(CH, P)
    slot = np.arange(E * TOK)
    arrays = {
        "x": i["x"].reshape(TOK, D),
        "ctx_t": i["ctx_768"].reshape(B * M, DC).T,
        "mask": i["mask_BxS2_bf1"].view(np.uint8),
        "mask_t": i["mask_BxS2_bf1"].view(np.uint8).T,
        "wq": rows_on_partitions(i["L0_xattn_Wq"]),
        "wk": i["L0_xattn_Wk"],
        "wv": i["L0_xattn_Wv"],
        "wo": rows_on_partitions(i["L0_xattn_Wo"]),
        "router": rows_on_partitions(i["L0_ffn_router_w"].T),
        "experts": np.stack(experts),
        "ident": np.eye(P, dtype=np.float32),
        "head_sel": (np.arange(P)[:, None] // HD == np.arange(HH)).astype(np.float32),
        "val_sel": np.stack([((row // M - np.array(FIRST_HEAD)[:, None] == j) & (row < SC)).T for j in range(HMAX)],
                            axis=2).astype(np.float32),
        "upper": (np.arange(P)[:, None] < np.arange(P)).astype(np.float32),
        "expert_no": np.broadcast_to(np.stack([np.arange(E) * TOK, E - np.arange(E)]), (P, 2, E)).astype(np.float32),
        "token_no": (np.arange(TILES + 1) * P + np.arange(P)[:, None]).astype(np.int32),
        "pads": np.stack([TOK + slot % P, 0 * slot], axis=1).astype(np.int32),
    }
    nc = bacc.Bacc("TRN2", target_bir_lowering=False, num_devices=1)
    feeds, args = {}, []
    for name, a in arrays.items():
        feeds[f"in_{name}"] = np.ascontiguousarray(a)
        args.append(nc.dram_tensor(f"in_{name}", a.shape, mybir.dt.from_np(a.dtype), kind="ExternalInput").ap())
    args.append(nc.dram_tensor("out_rows", (TOK + P, D), F32, kind="ExternalOutput").ap())
    program(nc, *args)
    result = run_bass_kernel_spmd(nc, [feeds], core_ids=[0])
    return result.results[0]["out_rows"][:TOK].reshape(B, N, D)
```

```python
import concourse.bass as bass
from concourse import mybir
from contextlib import ExitStack

F32 = mybir.dt.float32
F32R = mybir.dt.float32r
I32 = mybir.dt.int32
U8 = mybir.dt.uint8
BF16 = mybir.dt.bfloat16
ACT = mybir.ActivationFunctionType
ALU = mybir.AluOpType
AX = mybir.AxisListType

P = 128
B, N, D = 4, 1024, 256
M, DC = 77, 192
H, HD = 16, 16
F, E = 1024, 7
TOK = B * N
TILES = TOK // P
TPB_LOG = 3
KT = D // P
HH = H // 2
SC = HH * M
CH = -(-SC // P)
SCP = CH * P
VW = HD + 1
FIRST_HEAD = [c * P // M for c in range(CH)]
HEADS_IN = [min(HH - 1, (c * P + P - 1) // M) - c * P // M + 1 for c in range(CH)]
HMAX = max(HEADS_IN)
BLK = 256
NBLK = TOK // BLK
FT = F // P
WCOLS = 3 * KT * F
EPS_LN = 1e-5
EPS_TOP = 1e-9
UNROLL = 4
LX = 3
PIECE = WCOLS // TILES
WCH = 1024
NW = WCOLS // WCH
GU_CHUNKS = 2 * KT * F // WCH
VCOLS = CH * HMAX * VW
ARENA = (UNROLL + 4) * D + KT * P + 2 * KT * SCP
CONST_COLS = [P, KT * D, KT * D, KT * E, HH, CH * HMAX, P, 2 * E]
CONST_LOADS, CTX_LOADS = 2, 3
ROUTE_AT = 3


def cut(o, n):
    return slice(o, o + n)


def bc(ap, axis, n):
    a = ap.unsqueeze(axis)
    return a.to_broadcast([n if k == axis else s for k, s in enumerate(a.shape)])


def program(nc, x, ctx_w, mask, mask_t, experts, consts, token_no, pads, out):
    xn2_d = nc.dram_tensor("xn2_d", (TOK + P, D), F32, kind="Internal").ap()
    x1_d = nc.dram_tensor("x1_d", (TOK, D), F32, kind="Internal").ap()
    val_d = nc.dram_tensor("val_d", (B * KT, SCP, VW), F32, kind="Internal").ap()
    table_d = nc.dram_tensor("table_d", (E * TOK, 2), I32, kind="Internal").ap()

    with ExitStack() as stack:
        def sb(name, shape, dt=F32):
            return stack.enter_context(nc.sbuf_tensor(name, shape, dt))

        def sem(name):
            return stack.enter_context(nc.semaphore(name))

        def sems(name, n):
            return [sem(f"{name}{k}") for k in range(n)]

        consts_s = sb("consts_s", [P, sum(CONST_COLS)])
        ends = [sum(CONST_COLS[:k + 1]) for k in range(len(CONST_COLS))]
        ident_s, wq_f, wo_f, wr_f, head_s, valsel_f, upper_f, expert_f = (
            consts_s[:, cut(e - n, n)] for e, n in zip(ends, CONST_COLS))
        wq_s, wo_s, wr_s, expert_s = (a.rearrange("p (k n) -> p k n", k=2) for a in (wq_f, wo_f, wr_f, expert_f))
        valsel_s = valsel_f.rearrange("p (c j) -> p c j", c=CH)
        arena = sb("arena", [P, ARENA])
        taken = {"A": 0, "B": 0}

        def part(phase, *shape):
            n = 1
            for k in shape:
                n *= k
            o = taken[phase]
            taken[phase] = o + n
            assert taken[phase] <= ARENA
            ap = arena[:, cut(o, n)]
            if len(shape) == 2:
                ap = ap.rearrange("p (a b) -> p a b", a=shape[0])
            return ap

        xa = part("A", UNROLL, D)
        xr = part("A", 2, D)
        xn = part("A", 2, D)
        xnT = part("A", KT, P)
        prob = part("A", KT, SCP)
        probT = part("A", KT, SCP)
        xin = part("B", 2, D)
        x1b = part("B", 2, D)
        y = part("B", 2, D)
        gate = part("B", 2, 2 * BLK)
        hid = part("B", FT, BLK)
        mv1 = sb("mv1", [P, 2, 3])
        mv2 = sb("mv2", [P, 2, 3])
        stat1 = sb("stat1", [P, 2, 6])
        stat2 = sb("stat2", [P, 2, 6])
        smax = sb("smax", [P, KT, HH])
        rsum = sb("rsum", [P, H])
        att = sb("att", [P, D])
        attT = sb("attT", [P, KT, P])
        x1 = sb("x1", [P, 2, D])
        xn2 = sb("xn2", [P, 2, D])
        xn2T = sb("xn2T", [P, KT, P])
        logits = sb("logits", [P, TILES, E])
        zero = sb("zero", [P, D])
        power = sb("power", [P, 1])
        upper_s = sb("upper_s", [P, P], BF16)
        ones_b = sb("ones_b", [P, P], BF16)
        masks_b = sb("masks_b", [P, TILES, E], BF16)
        before_b = sb("before_b", [P, TILES, E], BF16)
        total_b = sb("total_b", [P, E], BF16)
        token_s = sb("token_s", [P, TILES + 1], I32)
        pay = sb("pay", [P, 2, TILES, 2], I32)
        pos = sb("pos", [P, 2, TILES], I32)
        counts = sb("counts", [1, 3, 8], I32)
        routes = sb("routes", [P, 6 * TILES * E + 5 * TILES])

        def route_part(k):
            return routes[:, cut(k * TILES * E, TILES * E)].rearrange("p (t e) -> p t e", e=E)

        def route_col(k):
            return routes[:, cut(6 * TILES * E + k * TILES, TILES)]

        r_prob, r_sel, r_one, r_two, r_sum, r_pos = (route_part(k) for k in range(6))
        r_a, r_p1, r_p2, r_b, r_w = (route_col(k) for k in range(5))
        raw = sb("raw", [P, WCOLS])
        w_hi = [sb(f"w_hi{k}", [P, WCOLS], F32R) for k in range(2)]
        w_lo = [sb(f"w_lo{k}", [P, WCOLS], F32R) for k in range(2)]
        xT_hi = sb("xT_hi", [P, KT, BLK], F32R)
        xT_lo = sb("xT_lo", [P, KT, BLK], F32R)
        hid_hi = sb("hid_hi", [P, FT, BLK], F32R)
        hid_lo = sb("hid_lo", [P, FT, BLK], F32R)
        vals = sb("vals", [P, B, KT, VCOLS])
        val_c = sb("val_c", [P, B, KT, CH * VW])
        qT_hi, qT_lo = (sb(n, [P, KT * P], F32R) for n in ("qT_hi", "qT_lo"))
        hids = [a[:].rearrange("p f n -> p (f n)") for a in (hid_hi, hid_lo)]
        km_hi, km_lo = (a[:, cut(0, KT * B * M)].rearrange("p (k n) -> p k n", k=KT) for a in hids)
        keys_hi, keys_lo = (w[1][:, cut(0, B * KT * SC)].rearrange("p (b k n) -> p b k n", b=B, k=KT) for w in (w_hi, w_lo))
        slots_g = sb("slots_g", [P, 2, 2], I32)
        slots_m = sb("slots_m", [P, 2, 2], I32)
        rows_s = sb("rows_s", [P, 2], I32)
        ps = stack.enter_context(nc.psum_tensor("ps", [P, 8, 512], F32))
        S0, T0, T1, M1, M2 = 0, 4, 5, 6, 7
        XT_BANK, GATE, UP, Y_BANK, RANK = 0, 1, 3, 5, 7

        ctx_s = raw[:, cut(0, 2 * B * M)].rearrange("p (k n) -> p k n", k=2)
        wkv_s = raw[:, cut(2 * B * M, 4 * D)].rearrange("p (w k n) -> p w k n", w=2, k=2)
        keys_m, keep, drop, fill = (raw[:, cut(1664 + 2 * B * M * k, 2 * B * M)].rearrange("p (k n) -> p k n", k=2) for k in range(4))
        val_x = raw[:, cut(4160, B * H * VW)].rearrange("p (b n) -> p b n", b=B)
        scratch = sb("scratch", [P, 64])
        count, rcount, some, none = (scratch[:, cut(4 * k, 4)] for k in range(4))
        ksum, kmean = (scratch[:, cut(16 + 8 * k, 8)].rearrange("p (k b) -> p k b", k=KT) for k in range(2))
        keep_k, keep_v = (scratch[:, cut(32 + 4 * k, 4)] for k in range(2))
        mask_s = sb("mask_s", [P, B * M], U8)
        mask_k = sb("mask_k", [P, B], U8)

        ld_const, ld_ctx, ld_raw0, ld_pads = sem("ld_const"), sem("ld_ctx"), sem("ld_raw0"), sem("ld_pads")
        dv_zero, st_zero, dv_link, pe_keys, pe_vals, dv_keys = (sem(n) for n in ("dv_zero", "st_zero", "dv_link", "pe_keys", "pe_vals", "dv_keys"))
        dv_valx, st_val, ld_valc, dv_vals, dv_parts, po_lay = (sem(n) for n in ("dv_valx", "st_val", "ld_valc", "dv_vals", "dv_parts", "po_lay"))
        ld_xa, ld_xr = sems("ld_xa", UNROLL), sems("ld_xr", 2)
        st_x1, st_xn2 = sems("st_x1", 2), sems("st_xn2", 2)
        dv_bn1, dv_ag1, dv_bn2, dv_ag2 = (sem(n) for n in ("dv_bn1", "dv_ag1", "dv_bn2", "dv_ag2"))
        po_eps1, po_pow1, po_dev1, po_eps2, po_pow2, po_dev2 = (sem(n) for n in ("po_eps1", "po_pow1", "po_dev1", "po_eps2", "po_pow2", "po_dev2"))
        ac_xn, ac_xn2, po_whi, po_wlo = (sem(n) for n in ("ac_xn", "ac_xn2", "po_whi", "po_wlo"))
        pe_xt, pe_qp, pe_ot, pe_wo, pe_x2t, pe_r = (sem(n) for n in ("pe_xt", "pe_qp", "pe_ot", "pe_wo", "pe_x2t", "pe_r"))
        pe_s, pe_pta, pe_ptb, pe_pv = (sems(n, 2) for n in ("pe_s", "pe_pta", "pe_ptb", "pe_pv"))
        ac_xnt, ac_qt, ac_ont, ac_x2t = (sem(n) for n in ("ac_xnt", "ac_qt", "ac_ont", "ac_x2t"))
        ac_exp, ac_pt = sems("ac_exp", 2), sems("ac_pt", 2)
        dv_max, dv_sub, dv_pt, dv_ql = sems("dv_max", 2), sems("dv_sub", 2), sems("dv_pt", 2), sem("dv_ql")
        dv_rc, dv_norm, dv_x1, dv_l = (sem(n) for n in ("dv_rc", "dv_norm", "dv_x1", "dv_l"))
        dv_shifted, ac_route, dv_masks, pe_rank, dv_pos, dv_counts, st_table = (sem(n) for n in ("dv_shifted", "ac_route", "dv_masks", "pe_rank", "dv_pos", "dv_counts", "st_table"))
        b_xin, b_x1, b_out, b_gather, b_slots_g, b_held, b_add = (sem(n) for n in ("b_xin", "b_x1", "b_out", "b_gather", "b_slots_g", "b_held", "b_add"))
        b_t, b_xhi, b_xlo, b_y, b_ysb = (sem(n) for n in ("b_t", "b_xhi", "b_xlo", "b_y", "b_ysb"))
        b_g, b_u, b_silu, b_h, b_hhi, b_hlo = (sems(n, 4) for n in ("b_g", "b_u", "b_silu", "b_h", "b_hhi", "b_hlo"))
        ld_raw, b_whi, b_wlo = sem("ld_raw"), sem("b_whi"), sem("b_wlo")

        waited = {name: sem(f"{name}_waited") for name in ("DVE", "Pool", "SP")}

        block = stack.enter_context(nc.Block())

        def lay(eng, b, what, halves=range(KT)):
            for h in halves:
                if what == "values":
                    i = eng.tensor_tensor(vals[:, b, h, :].rearrange("p (c j w) -> p c j w", c=CH, j=HMAX),
                                          bc(val_c[:, b, h, :].rearrange("p (c w) -> p c w", c=CH), 2, HMAX),
                                          bc(valsel_s, 3, VW), ALU.mult)
                else:
                    for k_m, keys in ((km_hi, keys_hi), (km_lo, keys_lo)):
                        i = eng.tensor_tensor(keys[:, b, h, :].rearrange("p (h k) -> p h k", h=HH),
                                              bc(k_m[:, h, cut(b * M, M)].bitcast(F32), 1, HH), bc(head_s, 2, M), ALU.mult)
            return i

        def peeled(step, i, batch=False):
            step(i % UNROLL, lambda o: 0 <= i + o < TILES, lambda o: i + o, *([lambda o: (i + o) >> TPB_LOG] if batch else []))

        def phase_a(eng, step, first, last, with_batch=False):
            lo, hi = UNROLL, TILES - UNROLL
            for i in range(first, lo):
                peeled(step, i, with_batch)
            with eng.Fori(lo // UNROLL, hi // UNROLL) as u:
                t = u * UNROLL
                at = {o: eng.snap(t + o, min_val=lo + o, max_val=hi - UNROLL + o)
                      for o in range(-LX - 1, 2 * UNROLL)}
                if with_batch:
                    of_body = eng.snap(u >> 1, min_val=0, max_val=B - 1)
                    before = eng.snap((t - 1) >> TPB_LOG, min_val=0, max_val=B - 1)
                    batches = {-1: before, **{o: of_body for o in range(UNROLL)}}
                for j in range(UNROLL):
                    step(j, lambda o: True, lambda o, j=j: at[j + o], *([lambda o, j=j: batches[j + o]] if with_batch else []))
            for i in range(hi, last + 1):
                peeled(step, i, with_batch)

        def uses(tile, slot, ring):
            return ((tile - slot) >> (ring.bit_length() - 1)) + 1

        def routed(eng, begin, after_first, finish):
            g = eng.alloc_register(f"{eng.engine.name}_g")

            def next_block(e, b, was, now, v=None):
                n = eng.snap(g, min_val=NBLK + 1, max_val=(E + 1) * NBLK - 1)
                begin(e, b, n, was, now, v)
                eng.reg_add(g, g, 1)

            def blocks(e, par):
                n = eng.value_load(counts[0:1, 0, bass.ds(e, 1)], min_val=1, max_val=NBLK)
                with eng.Fori(0, 3) as q:
                    with eng.If(q * 5 + 1 < n):
                        with eng.Fori(0, 5) as j:
                            b = eng.snap(q * 5 + j + 1, min_val=1, max_val=NBLK - 1)
                            with eng.If(b < n):
                                next_block(e, b, par, par)
                            eng.nop()
                    eng.nop()

            eng.wait_ge(dv_counts, 1)
            begin(0, 0, NBLK, 0, 1, None)
            eng.reg_mov(g, NBLK + 1)
            if after_first:
                after_first(0, 1, None)
            blocks(0, 1)
            with eng.Fori(0, (E - 1) // 2) as v:
                v = eng.snap(v, min_val=0, max_val=(E - 1) // 2 - 1)
                for k in range(2):
                    e = eng.snap(v * 2 + (1 + k), min_val=1 + k, max_val=E - 2 + k)
                    next_block(e, 0, 1 - k, k, v)
                    if after_first:
                        after_first(e, k, v)
                    blocks(e, k)
            finish(eng.snap(g, min_val=NBLK + E, max_val=(E + 1) * NBLK))

        def apart(eng):
            eng.sem_inc(waited[eng.engine.name], 1)

        def rows(ap, r, n=2):
            return ap[bass.ds(r, n * P), :].rearrange("(t p) d -> p t d", p=P)

        @block.sync
        def _(sp):
            sp.dma_start(consts_s[:], consts).then_inc(ld_const, 16)
            sp.dma_start(token_s[:], token_no).then_inc(ld_const, 16)
            for i in range(UNROLL):
                sp.dma_start(xa[:, i, :], x[cut(i * P, P), :]).then_inc(ld_xa[i], 16)
            sp.dma_start(table_d, pads).then_inc(ld_pads, 16)
            sp.wait_ge(dv_zero, 1)
            sp.dma_start(xn2_d[cut(TOK, P), :], zero[:]).then_inc(st_zero, 16)
            sp.dma_start(out[cut(TOK, P), :], zero[:]).then_inc(st_zero, 16)
            sp.dma_start(val_d[:, SC:, :].rearrange("b r w -> r b w"),
                         zero[0:SCP - SC, 0:B * KT * VW].rearrange("r (b w) -> r b w", w=VW)).then_inc(st_val, 16)
            sp.wait_ge(dv_valx, 1)
            for b in range(B):
                for h in range(KT):
                    sp.dma_start(val_d[b * KT + h, 0:SC, :].rearrange("(h k) c -> k h c", k=M),
                                 val_x[0:M, b, cut(h * HH * VW, HH * VW)].rearrange("k (h c) -> k h c", h=HH)).then_inc(st_val, 16)
            sp.wait_ge(st_val, 16 * (1 + B * KT))
            sp.dma_start(val_c[:].rearrange("p b k (c w) -> p (b k c) w", w=VW),
                         val_d.rearrange("g (c p) w -> p (g c) w", p=P)).then_inc(ld_valc, 16)
            sp.wait_ge(dv_vals, 1)
            sp.dma_start(raw[:], experts[0]).then_inc(ld_raw0, 16)

            def step(s, has, tile):
                if has(-2):
                    sp.wait_ge(dv_x1, tile(-2) + 1)
                if has(0):
                    sp.dma_start(xr[:, s % 2, :], x[bass.ds(tile(0) * P, P), :]).then_inc(ld_xr[s % 2], 16)
                if has(-2):
                    sp.dma_start(x1_d[bass.ds(tile(-2) * P, P), :], x1[:, s % 2, :]).then_inc(st_x1[s % 2], 16)
                    sp.wait_ge(ac_xn2, tile(-2) + 1)
                    sp.dma_start(xn2_d[bass.ds(tile(-2) * P, P), :], xn2[:, s % 2, :]).then_inc(st_xn2[s % 2], 16)
                if has(0) and has(UNROLL):
                    sp.wait_ge(ac_xn, tile(0) + 1)
                    sp.dma_start(xa[:, s, :], x[bass.ds(tile(UNROLL) * P, P), :]).then_inc(ld_xa[s], 16)

            phase_a(sp, step, 0, TILES)
            sp.wait_ge(ac_xn, TILES)
            for k in range(2):
                sp.wait_ge(st_x1[k], 16 * (TILES // 2 - k))
                sp.wait_ge(st_xn2[k], 16 * (TILES // 2 - k))
            sp.wait_ge(st_zero, 32)
            sp.dma_start(xin[:], rows(xn2_d, 0)).then_inc(b_xin, 16)
            sp.dma_start(x1b[:], rows(x1_d, 0)).then_inc(b_x1, 16)
            peeled(step, TILES + 1)
            for k in range(2):
                sp.wait_ge(st_x1[k], 16 * (TILES // 2))
                sp.wait_ge(st_xn2[k], 16 * (TILES // 2))
            sp.wait_ge(po_wlo, TILES)
            sp.dma_start(raw[:], experts[1]).then_inc(ld_raw, 16)

            sp.wait_ge(b_t, 1)
            sp.dma_start(xin[:], rows(xn2_d, BLK)).then_inc(b_xin, 16)
            with sp.Fori(1, NBLK - 1) as n:
                n = sp.snap(n, min_val=1, max_val=NBLK - 2)
                sp.wait_ge(b_ysb, n)
                sp.dma_start(rows(out, (n - 1) * BLK), y[:]).then_inc(b_out, 16)
                sp.dma_start(x1b[:], rows(x1_d, n * BLK)).then_inc(b_x1, 16)
                sp.wait_ge(b_t, n + 1)
                sp.dma_start(xin[:], rows(xn2_d, (n + 1) * BLK)).then_inc(b_xin, 16)
            sp.wait_ge(b_ysb, NBLK - 1)
            sp.dma_start(rows(out, (NBLK - 2) * BLK), y[:]).then_inc(b_out, 16)
            sp.dma_start(x1b[:], rows(x1_d, (NBLK - 1) * BLK)).then_inc(b_x1, 16)

            def begin(e, b, g, was, now, v):
                if isinstance(g, int):
                    sp.wait_ge(st_table, 16 * 2 * (TILES - 1))
                    sp.wait_ge(b_add, 32)
                    sp.dma_start(slots_g[:], rows(table_d, 0)).then_inc(b_slots_g, 16)
                    sp.wait_ge(b_ysb, NBLK)
                    sp.dma_start(rows(out, (NBLK - 1) * BLK), y[:]).then_inc(b_out, 16)
                    return
                row = sp.snap(e * TOK + b * BLK, min_val=BLK, max_val=E * TOK - BLK)
                sp.wait_ge(b_gather, (g - NBLK) * 32)
                sp.wait_ge(b_held, g - NBLK)
                sp.dma_start(slots_g[:], rows(table_d, row)).then_inc(b_slots_g, 16)

            def finish(g):
                sp.wait_ge(b_out, 16 * NBLK)
                sp.wait_ge(b_add, (g - NBLK) * 32 + 64)
                apart(sp)

            routed(sp, begin, None, finish)

        @block.gpsimd
        def _(po):
            def deviation(mv, s_eps, s_pow, s_dev, n):
                po.tensor_scalar(mv[:, 1:2], mv[:, 1:2], EPS_LN, None, ALU.add).then_inc(s_eps, 1)
                po.wait_ge(s_eps, n)
                po.tensor_tensor(mv[:, 1:2], mv[:, 1:2], power[:], ALU.pow).then_inc(s_pow, 1)
                po.wait_ge(s_pow, n)
                apart(po)
                po.tensor_scalar(mv[:, 2:3], mv[:, 0:1], mv[:, 1:2], -1.0, ALU.mult, ALU.mult).then_inc(s_dev, 1)

            po.memset(prob[:, :, SC:], 0.0).then_inc(po_lay, 1)
            po.wait_ge(dv_zero, 1)

            def step(s, has, tile):
                if has(-2):
                    po.wait_ge(dv_ag2, tile(-2) + 1)
                    apart(po)
                    deviation(mv2[:, s % 2, :], po_eps2, po_pow2, po_dev2, tile(-2) + 1)
                if has(2):
                    po.wait_ge(dv_ag1, tile(2) + 1)
                    apart(po)
                    deviation(mv1[:, s % 2, :], po_eps1, po_pow1, po_dev1, tile(2) + 1)
                if has(0) and isinstance(tile(0), int) and 1 <= tile(0) < B:
                    if tile(0) == 1:
                        po.wait_ge(dv_parts, 1)
                        po.wait_ge(ld_valc, 16)
                    lay(po, tile(0), "keys")
                    lay(po, tile(0), "values").then_inc(po_lay, 1)
                if has(-2):
                    o = tile(-2) * PIECE
                    if isinstance(o, int) and o == 0:
                        po.wait_ge(ld_raw0, 16)
                    po.tensor_copy(w_hi[0][:, bass.ds(o, PIECE)], raw[:, bass.ds(o, PIECE)]).then_inc(po_whi, 1)
                    po.wait_ge(po_whi, tile(-2) + 1)
                    po.tensor_tensor(w_lo[0][:, bass.ds(o, PIECE)], raw[:, bass.ds(o, PIECE)],
                                     w_hi[0][:, bass.ds(o, PIECE)].bitcast(F32), ALU.subtract).then_inc(po_wlo, 1)

            phase_a(po, step, -2, TILES + 1)

            po.wait_ge(dv_pos, 1)
            po.wait_ge(ld_pads, 16)
            for t in range(TILES):
                for k in range(2):
                    po.indirect_dma_start(out=table_d, out_offset=bass.IndirectOffsetOnAxis(ap=pos[:, k, t:t + 1], axis=0),
                                          in_=pay[:, k, t, :], in_offset=None).then_inc(st_table if t < TILES - 1 else b_add, 16)

            def add(g, t):
                po.wait_ge(b_ysb, g - 1)
                po.wait_ge(b_add, (g - NBLK) * 32 + 16 * t)
                apart(po)
                po.indirect_dma_start(out=out, out_offset=bass.IndirectOffsetOnAxis(ap=rows_s[:, t:t + 1], axis=0),
                                      in_=y[:, t, :], in_offset=None, compute_op=ALU.add).then_inc(b_add, 16)

            def begin(e, b, g, was, now, v):
                if not isinstance(g, int):
                    add(g, 0)
                po.wait_ge(b_slots_g, (g - NBLK) * 16 + 16)
                po.wait_ge(b_t, g)
                apart(po)
                for t in range(2):
                    po.indirect_dma_start(out=xin[:, t, :], out_offset=None, in_=xn2_d,
                                          in_offset=bass.IndirectOffsetOnAxis(ap=slots_g[:, t, 0:1], axis=0)).then_inc(b_gather, 16)
                if not isinstance(g, int):
                    add(g, 1)

            def finish(g):
                for n in (g, g + 1):
                    for t in range(2):
                        add(n, t)

            def outputs_written(e, par, v):
                if v is None:
                    po.wait_ge(b_out, 16 * NBLK)
                    po.wait_ge(st_zero, 32)

            routed(po, begin, outputs_written, finish)

        @block.tensor
        def _(pe):
            mm = nc.tensor.matmul

            pe.wait_ge(ld_ctx, 16 * CTX_LOADS)
            for b in range(B):
                for k, kp in ((0, P), (1, DC - P)):
                    last = mm(ps[0:M, 2 + b, 0:D], ctx_s[0:kp, k, cut(b * M, M)], wkv_s[0:kp, 1, k, :],
                              start=k == 0, stop=k == 1)
            last.then_inc(pe_vals, 1)
            for h in range(KT):
                for k, kp in ((0, P), (1, DC - P)):
                    last = mm(ps[:, h, 0:B * M], wkv_s[0:kp, 0, k, cut(h * P, P)], ctx_s[0:kp, k, :],
                              start=k == 0, stop=k == 1)
            last.then_inc(pe_keys, 1)
            pe.wait_ge(ld_const, 16 * CONST_LOADS)
            pe.wait_ge(po_lay, 1)

            def transpose_probs(half, chunks):
                for c in chunks:
                    bank, col = (T0, c * P) if c < 3 else (T1, (c - 3) * P)
                    i = nc.tensor.transpose(ps[:, bank, cut(col, P)], prob[:, half, cut(c * P, P)], ident_s)
                i.then_inc((pe_pta if bank == T0 else pe_ptb)[half], 1)

            def of_batch(a, batch, half, columns):
                return a[:, batch, half, columns] if isinstance(batch, int) else a[:, bass.ds(batch, 1), half, columns]

            def attend(half, batch):
                for c in range(CH):
                    n = HEADS_IN[c] * VW
                    i = mm(ps[:, M2, cut((half * HH + FIRST_HEAD[c]) * VW, n)], probT[:, half, cut(c * P, P)],
                           of_batch(vals, batch, half, cut(c * HMAX * VW, n)),
                           start=half == 0 and c == 0, stop=half == 1 and c == CH - 1, skip_group_check=True)
                i.then_inc(pe_pv[half], 1)

            def score(half, batch):
                n = SC // 2
                for q in range(2):
                    for k, (a, b) in enumerate(((qT_hi, keys_hi), (qT_lo, keys_hi), (qT_hi, keys_lo))):
                        i = mm(ps[:, S0 + 2 * half + q, 0:n], a[:, cut(half * P, P)], of_batch(b, batch, half, cut(q * n, n)),
                               start=k == 0, stop=k == 2)
                i.then_inc(pe_s[half], 1)

            def query(half):
                for k in range(KT):
                    i = mm(ps[:, M1, cut(D + half * P, P)], wq_s[:, k, cut(half * P, P)], xnT[:, k, :],
                           start=k == 0, stop=k == KT - 1)
                return i

            def transpose_rows(dst, src):
                for k in range(KT):
                    i = nc.tensor.transpose(dst[:, cut(k * P, P)], src[:, cut(k * P, P)], ident_s)
                return i

            def step(s, has, tile, batch):
                if has(-1):
                    before = batch(-1)
                    pe.wait_ge(ac_exp[1], tile(-1) + 1)
                    pe.wait_ge(ac_pt[0], tile(-1) + 1)
                    pe.wait_ge(dv_pt[0], tile(-1) + 1)
                    transpose_probs(1, range(3))
                    transpose_probs(1, range(3, CH))
                if has(-LX):
                    pe.wait_ge(ac_xn2, tile(-LX) + 1)
                    if has(0):
                        pe.wait_ge(dv_ql, tile(0) + 1)
                    transpose_rows(ps[:, M1, 0:D], xn2[:, (s - LX) % 2, :]).then_inc(pe_x2t, 1)
                if has(0):
                    now = batch(0)
                    pe.wait_ge(ac_qt, tile(0) + 1)
                    pe.wait_ge(dv_ql, tile(0) + 1)
                    if not isinstance(now, int) and s == 0:
                        pe.wait_ge(po_lay, now + 1)
                    if isinstance(now, int) and tile(0) == 0:
                        pe.wait_ge(dv_keys, 1)
                        pe.wait_ge(dv_valx, 1)
                    score(0, now)
                if has(-1):
                    if has(-2):
                        pe.wait_ge(dv_x1, tile(-2) + 1)
                    if has(-LX - 1):
                        pe.wait_ge(dv_l, tile(-LX - 1) + 1)
                    if isinstance(before, int) and tile(-1) == 0:
                        pe.wait_ge(dv_vals, 1)
                    attend(0, before)
                    pe.wait_ge(ac_pt[1], tile(-1) + 1)
                    pe.wait_ge(dv_pt[1], tile(-1) + 1)
                    attend(1, before)
                if has(1):
                    pe.wait_ge(ac_xn, tile(1) + 1)
                    if has(-LX):
                        pe.wait_ge(ac_x2t, tile(-LX) + 1)
                    transpose_rows(ps[:, M1, 0:D], xn[:, (s + 1) % 2, :]).then_inc(pe_xt, 1)
                if has(0):
                    if isinstance(now, int) and tile(0) == 0:
                        pe.wait_ge(dv_keys, 2)
                    score(1, now)
                if has(1):
                    pe.wait_ge(ac_xnt, tile(1) + 1)
                    query(0)
                if has(0):
                    pe.wait_ge(ac_exp[0], tile(0) + 1)
                    transpose_probs(0, range(3))
                if has(-1):
                    pe.wait_ge(dv_norm, tile(-1) + 1)
                    transpose_rows(ps[:, T1, D:2 * D], att[:]).then_inc(pe_ot, 1)
                if has(1):
                    query(1).then_inc(pe_qp, 1)
                if has(-LX):
                    pe.wait_ge(ac_x2t, tile(-LX) + 1)
                    if not has(-1):
                        if has(-LX - 1):
                            pe.wait_ge(dv_l, tile(-LX - 1) + 1)
                            pe.wait_ge(dv_x1, tile(-2) + 1 if has(-2) else TILES)
                    for k in range(KT):
                        last = mm(ps[:, M2, cut(2 * D - 8, E)], xn2T[:, k, :], wr_s[:, k, :],
                                  start=k == 0, stop=k == KT - 1)
                    last.then_inc(pe_r, 1)
                if has(0):
                    if has(-1):
                        pe.wait_ge(ac_ont, tile(-1) + 1)
                    transpose_probs(0, range(3, CH))
                if has(-1):
                    pe.wait_ge(ac_ont, tile(-1) + 1)
                    for k in range(KT):
                        last = mm(ps[:, M2, 0:D], attT[:, k, :], wo_s[:, k, :], start=k == 0, stop=k == KT - 1)
                    last.then_inc(pe_wo, 1)

            phase_a(pe, step, -1, TILES + LX - 2, with_batch=True)

            def transpose_block(g, wait):
                wait()
                if not (isinstance(g, int) and g == 0):
                    pe.wait_ge(b_xlo, g)
                for k in range(KT):
                    for t in range(2):
                        i = nc.tensor.transpose(ps[:, XT_BANK, cut(k * BLK + t * P, P)], xin[:, t, cut(k * P, P)], ident_s)
                i.then_inc(b_t, 1)

            def down(g, par):
                if not (isinstance(g, int) and g == 1):
                    pe.wait_ge(b_ysb, g - 1)
                for p in range(4):
                    pe.wait_ge(b_hhi[p], g)
                    pe.wait_ge(b_hlo[p], g)
                    for t in range(2):
                        for f in (2 * p, 2 * p + 1):
                            o = 2 * KT * F + f * D
                            for n, (a, w) in enumerate(((hid_hi, w_hi), (hid_lo, w_hi), (hid_hi, w_lo))):
                                i = mm(ps[:, Y_BANK + t, 0:D], a[:, f, cut(t * P, P)], w[par][:, cut(o, D)],
                                       start=f == 0 and n == 0, stop=f == FT - 1 and n == 2)
                i.then_inc(b_y, 1)

            def gate_up(g, par):
                pe.wait_ge(b_xlo, g + 1)
                for p in range(4):
                    if p >= 2:
                        pe.wait_ge(b_h[p - 2], g + 1)
                    for m, (bank, ready) in enumerate(((GATE + p % 2, b_g[p]), (UP + p % 2, b_u[p]))):
                        for f in range(2):
                            for k in range(KT):
                                o = (m * KT + k) * F + (2 * p + f) * P
                                for n, (w, a) in enumerate(((w_hi, xT_hi), (w_hi, xT_lo), (w_lo, xT_hi))):
                                    i = mm(ps[:, bank, cut(f * BLK, BLK)], w[par][:, cut(o, P)], a[:, k, :],
                                           start=k == 0 and n == 0, stop=k == KT - 1 and n == 2)
                        i.then_inc(ready, 1)

            def shared(g):
                transpose_block(g, lambda: pe.wait_ge(b_xin, g * 16 + 16))
                down(g, 0)
                gate_up(g, 0)

            transpose_block(0, lambda: pe.wait_ge(b_xin, 16))
            peeled(step, TILES + LX - 1, batch=True)
            pe.wait_ge(po_wlo, TILES)
            gate_up(0, 0)
            for g in range(1, ROUTE_AT):
                shared(g)
            pe.wait_ge(dv_masks, 1)
            mm(ps[:, RANK, 0:TILES * E], upper_s[:], masks_b[:].rearrange("p t e -> p (t e)"), start=True, stop=False)
            mm(ps[:, RANK, 0:TILES * E], ones_b[:], before_b[:].rearrange("p t e -> p (t e)"), start=False, stop=True)
            mm(ps[:, RANK, cut(TILES * E, E)], ones_b[:], total_b[:], start=True, stop=True).then_inc(pe_rank, 1)
            shared(ROUTE_AT)
            with pe.Fori(ROUTE_AT + 1, NBLK) as g:
                shared(pe.snap(g, min_val=ROUTE_AT + 1, max_val=NBLK - 1))

            def begin(e, b, g, was, now, v):
                transpose_block(g, lambda: pe.wait_ge(b_gather, (g - NBLK) * 32 + 32))
                down(g, was)
                if isinstance(b, int):
                    pe.wait_ge(b_wlo, (e + 1) * NW)
                gate_up(g, now)

            routed(pe, begin, None, lambda g: down(g, 1))

        @block.scalar
        def _(ac):
            for dst, src in ((raw[:, cut(0, 2 * B * M + 4 * D)], ctx_w),
                             (mask_s[:], mask.rearrange("b k -> (b k)").unsqueeze(0).partition_broadcast(P)),
                             (mask_k[0:M, :], mask_t)):
                ac.dma_start(dst, src).then_inc(ld_ctx, 16)

            def copy(dst, src):
                return nc.scalar.activation(dst, src, ACT.Copy)

            def soften(half, n):
                ac.wait_ge(dv_sub[half], n)
                nc.scalar.activation(prob[:, half, 0:SC], prob[:, half, 0:SC], ACT.Exp, scale=HD ** -0.5).then_inc(ac_exp[half], 1)

            def probs_a(half, n):
                ac.wait_ge(pe_pta[half], n)
                copy(probT[:, half, 0:3 * P], ps[:, T0, 0:3 * P]).then_inc(ac_pt[half], 1)

            def normalise(dst, src, mv):
                return nc.scalar.activation(dst, src, ACT.Identity, bias=mv[:, 2:3], scale=mv[:, 1:2])

            def step(s, has, tile):
                if has(-1):
                    probs_a(1, tile(-1) + 1)
                if has(-LX):
                    ac.wait_ge(pe_x2t, tile(-LX) + 1)
                    copy(xn2T[:].rearrange("p k n -> p (k n)"), ps[:, M1, 0:D]).then_inc(ac_x2t, 1)
                if has(1):
                    ac.wait_ge(pe_xt, tile(1) + 1)
                    copy(xnT[:].rearrange("p k n -> p (k n)"), ps[:, M1, 0:D]).then_inc(ac_xnt, 1)
                if has(0):
                    soften(0, tile(0) + 1)
                if has(-1):
                    ac.wait_ge(pe_ot, tile(-1) + 1)
                    copy(attT[:].rearrange("p k n -> p (k n)"), ps[:, T1, D:2 * D]).then_inc(ac_ont, 1)
                if has(1):
                    ac.wait_ge(pe_qp, tile(1) + 1)
                    copy(qT_hi[:], ps[:, M1, D:2 * D]).then_inc(ac_qt, 1)
                if has(0):
                    soften(1, tile(0) + 1)
                    probs_a(0, tile(0) + 1)
                if has(-2):
                    ac.wait_ge(po_dev2, tile(-2) + 1)
                    if has(-4):
                        ac.wait_ge(pe_x2t, tile(-4) + 1)
                        ac.wait_ge(st_xn2[s % 2], uses(tile(-4), s % 2, 2) * 16)
                    normalise(xn2[:, s % 2, :], x1[:, s % 2, :], mv2[:, s % 2, :]).then_inc(ac_xn2, 1)
                if has(2):
                    ac.wait_ge(po_dev1, tile(2) + 1)
                    if has(0):
                        ac.wait_ge(pe_xt, tile(0) + 1)
                    normalise(xn[:, s % 2, :], xa[:, (s + 2) % UNROLL, :], mv1[:, s % 2, :]).then_inc(ac_xn, 1)

            phase_a(ac, step, -2, TILES + LX - 2)

            def x_high(g):
                ac.wait_ge(b_t, g + 1)
                copy(xT_hi[:].rearrange("p k n -> p (k n)"), ps[:, XT_BANK, :]).then_inc(b_xhi, 1)

            def act_block(g, early=None, late=None):
                if not (isinstance(g, int) and g == 0):
                    x_high(g)
                if early:
                    early()

                def high(p):
                    ac.wait_ge(b_h[p], g + 1)
                    copy(hid_hi[:, cut(2 * p, 2), :], hid[:, cut(2 * p, 2), :]).then_inc(b_hhi[p], 1)

                for p in range(4):
                    ac.wait_ge(b_g[p], g + 1)
                    if p >= 2:
                        ac.wait_ge(b_h[p - 2], g + 1)
                    nc.scalar.activation(gate[:, p % 2, :], ps[:, GATE + p % 2, :], ACT.Silu).then_inc(b_silu[p], 1)
                    if p:
                        high(p - 1)
                    if late:
                        late(p)
                high(3)

            def high_weights(par, chunks):
                for c in chunks:
                    copy(w_hi[par][:, cut(c * WCH, WCH)], raw[:, cut(c * WCH, WCH)]).then_inc(b_whi, 1)

            def load_raw(at):
                ac.wait_ge(b_wlo, (at - 1) * NW)
                if not isinstance(at, int):
                    at = nc.s_assert_within(at, 0, E, skip_runtime_bounds_check_because="the last body's load is left out")
                ac.dma_start(raw[:], experts[bass.ds(at, 1)].rearrange("a p n -> p (a n)")).then_inc(ld_raw, 16)

            def soften_routes(p):
                if p == 0:
                    ac.wait_ge(dv_shifted, 1)
                    nc.scalar.activation(r_prob, r_prob, ACT.Exp).then_inc(ac_route, 1)

            def first_weights():
                ac.wait_ge(ld_raw, 16)
                high_weights(1, range(NW))

            x_high(0)
            peeled(step, TILES + LX - 1)
            act_block(0, late=soften_routes)
            act_block(1)
            act_block(2, early=first_weights)
            load_raw(2)
            with ac.Fori(ROUTE_AT, NBLK) as g:
                act_block(ac.snap(g, min_val=ROUTE_AT, max_val=NBLK - 1))

            def begin(e, b, g, was, now, v):
                if not (isinstance(b, int) and b == 0):
                    return act_block(g)
                unless_last = v is not None and now == 1

                def guarded(part):
                    if unless_last:
                        with ac.If(v < (E - 1) // 2 - 1):
                            part()
                        ac.nop()
                    else:
                        part()

                def early():
                    ac.wait_ge(ld_raw, (e + 2) * 16)
                    ac.wait_ge(b_u[3], g)
                    high_weights(was, range(GU_CHUNKS))

                def late(p):
                    if p == 1:
                        def part():
                            ac.wait_ge(b_y, g)
                            high_weights(was, range(GU_CHUNKS, NW))
                        guarded(part)

                act_block(g, early=lambda: guarded(early), late=late)
                if v is None:
                    load_raw(e + 3)
                else:
                    with ac.If(v < (E - 1) // 2 - 1):
                        load_raw(e + 3)
                    ac.nop()

            routed(ac, begin, None, lambda g: None)

        @block.vector
        def _(dv):
            V = nc.vector
            links = [0]

            def link(i):
                links[0] += 1
                i.then_inc(dv_link, 1)
                dv.wait_ge(dv_link, links[0])

            V.memset(power[:], -0.5)
            V.memset(zero[:], 0.0).then_inc(dv_zero, 1)
            V.memset(ones_b[:], 1.0)
            dv.wait_ge(ld_const, 16 * CONST_LOADS)
            V.tensor_copy(upper_s[:], upper_f)
            for t in range(2):
                V.tensor_copy(rows_s[:, t:t + 1], token_s[:, TILES:TILES + 1])

            def key_values():
                dv.wait_ge(ld_ctx, 16 * CTX_LOADS)
                V.tensor_copy(keep_k[0:M], mask_k[0:M])
                for h in range(KT):
                    i = V.tensor_copy(keep[:, h, :], mask_s[:])
                link(i)
                V.tensor_scalar(drop, keep, -1.0, 1.0, ALU.mult, ALU.add)
                link(V.tensor_reduce(count, keep[:, 0, :].rearrange("p (b k) -> p b k", b=B), AX.X, ALU.add))
                V.tensor_scalar(some, count, 1.0, None, ALU.min)
                link(V.tensor_scalar(count, count, 1.0, None, ALU.max))
                V.reciprocal(rcount, count)
                link(V.tensor_scalar(none, some, -1.0, 1.0, ALU.mult, ALU.add))
                link(V.tensor_tensor(keep_v[0:M], keep_k[0:M], none[0:M], ALU.max))
                dv.wait_ge(pe_vals, 1)
                for b in range(B):
                    by_head = val_x[0:M, b, :].rearrange("k (h c) -> k h c", h=H)
                    V.tensor_scalar(by_head[:, :, 0:HD], ps[0:M, 2 + b, 0:D].rearrange("k (h c) -> k h c", h=H),
                                    keep_v[0:M, b:b + 1], None, ALU.mult)
                    i = V.tensor_copy(by_head[:, :, HD:], bc(keep_v[0:M, b:b + 1].to_broadcast([M, H]), 2, VW - HD))
                i.then_inc(dv_valx, 1)
                dv.wait_ge(pe_keys, 1)
                by_batch = [a.rearrange("p k (b m) -> p (k b) m", b=B) for a in (keys_m, drop, fill)]
                link(V.tensor_tensor(keys_m, ps[:, 0:KT, 0:B * M], keep, ALU.mult))
                link(V.tensor_reduce(ksum.rearrange("p k b -> p (k b)"), by_batch[0], AX.X, ALU.add))
                link(V.tensor_tensor(kmean, ksum, bc(rcount, 1, KT), ALU.mult))
                link(V.tensor_tensor(by_batch[2], by_batch[1], bc(kmean.rearrange("p k b -> p (k b)"), 2, M), ALU.mult))
                link(V.tensor_tensor(keys_m, keys_m, fill, ALU.add))
                link(V.tensor_copy(km_hi, keys_m))
                i = V.tensor_tensor(km_lo, keys_m, km_hi.bitcast(F32), ALU.subtract)
                i.then_inc(dv_parts, 1)
                dv.wait_ge(dv_parts, 1)
                for h in range(KT):
                    lay(V, 0, "keys", [h]).then_inc(dv_keys, 1)

            def chunk_values():
                dv.wait_ge(ld_valc, 16)
                lay(V, 0, "values").then_inc(dv_vals, 1)

            def norm_stats(src, stat, mv, s_bn, s_ag, n):
                V.bn_stats(stat, src).then_inc(s_bn, 1)
                dv.wait_ge(s_bn, n)
                apart(dv)
                V.bn_aggr(mv[:, 0:2], stat).then_inc(s_ag, 1)

            def shift(half, n):
                scores = ps[:, cut(S0 + 2 * half, 2), 0:SC // 2].rearrange("p q (h k) -> p q h k", k=M)
                top = smax[:, half, :].rearrange("p (q h) -> p q h", q=2)
                dv.wait_ge(pe_s[half], n)
                V.tensor_reduce(top, scores, AX.X, ALU.max).then_inc(dv_max[half], 1)
                dv.wait_ge(dv_max[half], n)
                V.tensor_tensor(prob[:, half, 0:SC].rearrange("p (q h k) -> p q h k", q=2, k=M), scores,
                                bc(top, 3, M), ALU.subtract).then_inc(dv_sub[half], 1)

            def probs_b(half, n):
                dv.wait_ge(pe_ptb[half], n)
                V.tensor_copy(probT[:, half, 3 * P:], ps[:, T1, 0:2 * P]).then_inc(dv_pt[half], 1)

            def queries_low(n):
                dv.wait_ge(ac_qt, n)
                V.tensor_tensor(qT_lo[:], ps[:, M1, D:2 * D], qT_hi[:].bitcast(F32), ALU.subtract).then_inc(dv_ql, 1)

            def step(s, has, tile):
                if has(-2):
                    n = tile(-2) + 1
                    dv.wait_ge(ld_xr[s % 2], uses(tile(-2), s % 2, 2) * 16)
                    if has(-4):
                        dv.wait_ge(st_x1[s % 2], uses(tile(-4), s % 2, 2) * 16)
                        dv.wait_ge(ac_xn2, tile(-4) + 1)
                    dv.wait_ge(pe_wo, n)
                    if has(-LX - 1):
                        dv.wait_ge(pe_r, tile(-LX - 1) + 1)
                    V.tensor_tensor(x1[:, s % 2, :], ps[:, M2, 0:D], xr[:, s % 2, :], ALU.add).then_inc(dv_x1, 1)
                if has(-LX - 1):
                    if not has(-2):
                        dv.wait_ge(pe_r, tile(-LX - 1) + 1)
                    V.tensor_copy(logits[:, bass.ds(tile(-LX - 1), 1), :].rearrange("p a e -> p (a e)"),
                                  ps[:, M2, cut(2 * D - 8, E)]).then_inc(dv_l, 1)
                if has(-2):
                    dv.wait_ge(dv_x1, n)
                    norm_stats(x1[:, s % 2, :], stat2[:, s % 2, :], mv2[:, s % 2, :], dv_bn2, dv_ag2, n)
                if has(-1):
                    probs_b(1, tile(-1) + 1)
                if has(0):
                    shift(0, tile(0) + 1)
                if has(-1):
                    heads = ps[:, M2, 0:H * VW].rearrange("p (h c) -> p h c", h=H)
                    dv.wait_ge(pe_pv[1], tile(-1) + 1)
                    V.reciprocal(rsum[:], heads[:, :, HD]).then_inc(dv_rc, 1)
                    dv.wait_ge(dv_rc, tile(-1) + 1)
                    V.tensor_tensor(att[:].rearrange("p (h c) -> p h c", h=H), heads[:, :, 0:HD],
                                    bc(rsum[:], 2, HD), ALU.mult).then_inc(dv_norm, 1)
                if has(0):
                    shift(1, tile(0) + 1)
                if has(2):
                    n = tile(2) + 1
                    dv.wait_ge(ld_xa[(s + 2) % UNROLL], uses(tile(2), (s + 2) % UNROLL, UNROLL) * 16)
                    if has(0):
                        dv.wait_ge(ac_xn, tile(0) + 1)
                    norm_stats(xa[:, (s + 2) % UNROLL, :], stat1[:, s % 2, :], mv1[:, s % 2, :], dv_bn1, dv_ag1, n)
                if has(1) and not has(0):
                    key_values()
                if has(1):
                    queries_low(tile(1) + 1)
                if has(0):
                    probs_b(0, tile(0) + 1)

            for i in (-2, -1):
                peeled(step, i)
            chunk_values()
            phase_a(dv, step, 0, TILES + LX - 1)

            def x_low(g):
                dv.wait_ge(b_xhi, g + 1)
                V.tensor_tensor(xT_lo[:].rearrange("p k n -> p (k n)"), ps[:, XT_BANK, :],
                                xT_hi[:].rearrange("p k n -> p (k n)").bitcast(F32), ALU.subtract).then_inc(b_xlo, 1)

            def block_of(g, finish, early=None, late=None):
                if not (isinstance(g, int) and g == 0):
                    x_low(g)
                if early:
                    early()
                if finish:
                    finish(g)

                def low(p):
                    dv.wait_ge(b_hhi[p], g + 1)
                    pair = cut(2 * p, 2)
                    V.tensor_tensor(hid_lo[:, pair, :], hid[:, pair, :], hid_hi[:, pair, :].bitcast(F32),
                                    ALU.subtract).then_inc(b_hlo[p], 1)

                for p in range(4):
                    dv.wait_ge(b_silu[p], g + 1)
                    dv.wait_ge(b_u[p], g + 1)
                    V.tensor_tensor(hid[:, cut(2 * p, 2), :].rearrange("p f n -> p (f n)"), gate[:, p % 2, :],
                                    ps[:, UP + p % 2, :], ALU.mult).then_inc(b_h[p], 1)
                    if p:
                        low(p - 1)
                    if late:
                        late(p)
                low(3)

            def end_shared(g):
                dv.wait_ge(b_y, g)
                dv.wait_ge(b_x1, g * 16)
                if not (isinstance(g, int) and g == 1):
                    dv.wait_ge(b_out, g * 16 - 16)
                V.tensor_tensor(y, ps[:, cut(Y_BANK, 2), 0:D], x1b, ALU.add).then_inc(b_ysb, 1)

            def end_routed(g):
                dv.wait_ge(b_y, g)
                dv.wait_ge(b_held, g - NBLK)
                dv.wait_ge(b_add, (g - NBLK) * 32 + 32)
                for t in range(2):
                    V.tensor_scalar(y[:, t, :], ps[:, Y_BANK + t, 0:D], slots_m[:, t, 1:2].bitcast(F32), None, ALU.mult)
                V.tensor_copy(rows_s[:], slots_m[:, :, 0]).then_inc(b_ysb, 1)

            def hold_slots(g):
                dv.wait_ge(b_slots_g, (g - NBLK) * 16 + 16)
                dv.wait_ge(b_ysb, g)
                V.tensor_copy(slots_m[:, :, 0], slots_g[:, :, 0])
                V.tensor_copy(slots_m[:, :, 1].bitcast(F32), slots_g[:, :, 1].bitcast(F32)).then_inc(b_held, 1)

            def end_and_hold(g):
                (end_shared if isinstance(g, int) else end_routed)(g)
                hold_slots(g)

            def low_weights(at, par, chunks):
                for c in chunks:
                    dv.wait_ge(b_whi, (at - 1) * NW + c + 1)
                    V.tensor_tensor(w_lo[par][:, cut(c * WCH, WCH)], raw[:, cut(c * WCH, WCH)],
                                    w_hi[par][:, cut(c * WCH, WCH)].bitcast(F32), ALU.subtract).then_inc(b_wlo, 1)

            rank = bc(expert_s[:, 1, :], 1, TILES)

            def best(top, one):
                link(V.tensor_reduce(top, r_prob, AX.X, ALU.max))
                link(V.tensor_tensor(r_sel, r_prob, bc(top, 2, E), ALU.is_equal))
                link(V.tensor_tensor(r_sel, r_sel, rank, ALU.mult))
                link(V.tensor_reduce(r_a, r_sel, AX.X, ALU.max))
                link(V.tensor_tensor(one, rank, bc(r_a, 2, E), ALU.is_equal))

            def choose_first(p):
                if p == 0:
                    dv.wait_ge(dv_l, TILES)
                    link(V.tensor_reduce(r_a, logits[:], AX.X, ALU.max))
                    V.tensor_tensor(r_prob, logits[:], bc(r_a, 2, E), ALU.subtract).then_inc(dv_shifted, 1)
                if p == 2:
                    dv.wait_ge(ac_route, 1)
                    link(V.tensor_reduce(r_a, r_prob, AX.X, ALU.add))
                    link(V.reciprocal(r_b, r_a))
                    link(V.tensor_tensor(r_prob, r_prob, bc(r_b, 2, E), ALU.mult))
                if p == 3:
                    best(r_p1, r_one)

            def choose_second(p):
                if p == 0:
                    link(V.scalar_tensor_tensor(r_prob, r_one, -2.0, r_prob, ALU.mult, ALU.add))
                    best(r_p2, r_two)
                if p == 1:
                    link(V.tensor_tensor(r_a, r_p1, r_p2, ALU.add))
                    link(V.tensor_scalar(r_a, r_a, EPS_TOP, None, ALU.add))
                    link(V.reciprocal(r_b, r_a))
                    for k, top in enumerate((r_p1, r_p2)):
                        V.tensor_tensor(pay[:, k, :, 1].bitcast(F32), top, r_b, ALU.mult)
                        V.tensor_copy(pay[:, k, :, 0], token_s[:, 0:TILES])
                    link(V.tensor_tensor(masks_b[:], r_one, r_two, ALU.add))
                if p == 2:
                    for e in range(E):
                        i = V.tensor_tensor_scan(r_sum[:, :, e], ones_b[:, 0:TILES], masks_b[:, :, e], 0.0, ALU.mult, ALU.add)
                    link(i)
                    V.tensor_copy(total_b[:], r_sum[:, TILES - 1, :])
                    V.tensor_tensor(before_b[:], r_sum, masks_b[:], ALU.subtract).then_inc(dv_masks, 1)

            def place():
                dv.wait_ge(pe_rank, 1)
                link(V.tensor_tensor(r_pos, ps[:, RANK, 0:TILES * E].rearrange("p (t e) -> p t e", e=E),
                                     bc(expert_s[:, 0, :], 1, TILES), ALU.add))
                for k, one in enumerate((r_one, r_two)):
                    link(V.tensor_tensor(r_sel, r_pos, one, ALU.mult))
                    link(V.tensor_reduce(r_a, r_sel, AX.X, ALU.add))
                    link(V.tensor_copy(pos[:, k, :], r_a))
                link(V.tensor_scalar(counts[0:1, 1, 0:E], ps[0:1, RANK, cut(TILES * E, E)], float(BLK - 1), None, ALU.add))
                link(V.tensor_single_scalar(counts[0:1, 2, 0:E], counts[0:1, 1, 0:E], BLK.bit_length() - 1, ALU.arith_shift_right))
                V.tensor_scalar(counts[0:1, 0, 0:E], counts[0:1, 2, 0:E], 1, None, ALU.max).then_inc(dv_counts, 1)
                V.tensor_copy(r_a[:, 0:1], r_b[:, 0:1]).then_inc(dv_pos, 1)

            x_low(0)
            peeled(step, TILES + LX)
            block_of(0, None, late=choose_first)
            block_of(1, end_shared, late=choose_second)
            block_of(2, end_shared, early=lambda: low_weights(1, 1, range(GU_CHUNKS)),
                     late=lambda p: low_weights(1, 1, range(GU_CHUNKS, NW)) if p == 1 else None)
            block_of(ROUTE_AT, end_shared, early=place)
            with dv.Fori(ROUTE_AT + 1, NBLK) as g:
                block_of(dv.snap(g, min_val=ROUTE_AT + 1, max_val=NBLK - 1), end_shared)

            def begin(e, b, g, was, now, v):
                if not (isinstance(b, int) and b == 0):
                    return block_of(g, end_and_hold)
                unless_last = v is not None and now == 1

                def guarded(part):
                    if unless_last:
                        with dv.If(v < (E - 1) // 2 - 1):
                            part()
                        dv.nop()
                    else:
                        part()

                def late(p):
                    if p == 1:
                        guarded(lambda: low_weights(e + 2, was, range(GU_CHUNKS, NW)))

                block_of(g, end_and_hold, early=lambda: guarded(lambda: low_weights(e + 2, was, range(GU_CHUNKS))), late=late)

            def y_stored(e, par, v):
                if v is None:
                    dv.wait_ge(b_out, 16 * NBLK)

            routed(dv, begin, y_stored, end_routed)


def kernel(**inputs):
    import numpy as np
    import concourse.bacc as bacc
    from concourse.bass_utils import run_bass_kernel_spmd

    def rows_on_partitions(w):
        return w.reshape(-1, P, w.shape[-1]).transpose(1, 0, 2)

    def padded(w):
        return rows_on_partitions(np.concatenate([w, np.zeros((2 * P - DC, w.shape[1]), w.dtype)])).reshape(P, -1)

    def expert(gate, up, down):
        return np.concatenate([rows_on_partitions(w.T).reshape(P, -1) for w in (gate, up, down)], axis=1)

    i = {k: np.asarray(v) for k, v in inputs.items()}
    experts = [expert(i["L0_ffn_shared_gate"], i["L0_ffn_shared_up"], i["L0_ffn_shared_down"])]
    experts += [expert(i["L0_ffn_routed_gate"][e], i["L0_ffn_routed_up"][e], i["L0_ffn_routed_down"][e]) for e in range(E)]
    row = np.arange(SCP).reshape(CH, P)
    slot = np.arange(E * TOK)
    arrays = {
        "x": i["x"].reshape(TOK, D),
        "ctx_w": np.concatenate([padded(i["ctx_768"].reshape(B * M, DC).T), padded(i["L0_xattn_Wk"]),
                                 padded(i["L0_xattn_Wv"])], axis=1),
        "mask": i["mask_BxS2_bf1"].view(np.uint8),
        "mask_t": i["mask_BxS2_bf1"].view(np.uint8).T,
        "experts": np.stack(experts),
        "consts": np.concatenate(
            [np.eye(P, dtype=np.float32)]
            + [rows_on_partitions(w).reshape(P, -1) for w in (i["L0_xattn_Wq"], i["L0_xattn_Wo"], i["L0_ffn_router_w"].T)]
            + [(np.arange(P)[:, None] // HD == np.arange(HH)).astype(np.float32),
               np.stack([((row // M - np.array(FIRST_HEAD)[:, None] == j) & (row < SC)).T for j in range(HMAX)],
                        axis=2).astype(np.float32).reshape(P, -1),
               (np.arange(P)[:, None] < np.arange(P)).astype(np.float32),
               np.broadcast_to(np.concatenate([np.arange(E) * TOK, E - np.arange(E)]), (P, 2 * E)).astype(np.float32)], axis=1),
        "token_no": (np.arange(TILES + 1) * P + np.arange(P)[:, None]).astype(np.int32),
        "pads": np.stack([TOK + slot % P, 0 * slot], axis=1).astype(np.int32),
    }
    nc = bacc.Bacc("TRN2", target_bir_lowering=False, num_devices=1)
    feeds, args = {}, []
    for name, a in arrays.items():
        feeds[f"in_{name}"] = np.ascontiguousarray(a)
        args.append(nc.dram_tensor(f"in_{name}", a.shape, mybir.dt.from_np(a.dtype), kind="ExternalInput").ap())
    args.append(nc.dram_tensor("out_rows", (TOK + P, D), F32, kind="ExternalOutput").ap())
    program(nc, *args)
    result = run_bass_kernel_spmd(nc, [feeds], core_ids=[0])
    return result.results[0]["out_rows"][:TOK].reshape(B, N, D)
```
